# Optimizing a Trainium2 kernel written in Bass

```python
import numpy as np
import jax
import jax.numpy as jnp

def _softmax(x, axis=-1):
    return jax.nn.softmax(x, axis=axis)

def _gelu(x):
    return jax.nn.gelu(x, approximate=True)

def _silu(x):
    return jax.nn.silu(x)

def _sigmoid(x):
    return jax.nn.sigmoid(x)

def _layernorm(x, axis=-1, eps=1e-05):
    m = jnp.mean(x, axis=axis, keepdims=True)
    v = jnp.var(x, axis=axis, keepdims=True)
    return (x - m) / jnp.sqrt(v + eps)

def _scatter_add(tgt, idx, src, axis=0):
    return tgt.at[idx].add(src)

def _segment_sum(src, seg, n):
    return jax.ops.segment_sum(src, seg, n)
kernel_name = 'mk_adaln_ffn_d2_seqx_r4_9238da'

def setup_inputs(seed: int=0):
    np.random.seed(seed)
    _w = jnp.asarray

    def _rec_inputs():
        import jax
        import jax.numpy as jnp
        _rk = jax.random.key(seed)
        x = -0.000125 + 0.9999 * jax.random.normal(jax.random.fold_in(_rk, 1), (64, 64, 1024), jnp.float32)
        _lenS = 64 - jax.random.randint(jax.random.fold_in(_rk, 7), (64,), 0, max(1, 64 // 4) + 1, jnp.int32)
        _lenS2 = 64 - jax.random.randint(jax.random.fold_in(_rk, 8), (64,), 0, max(1, 64 // 4) + 1, jnp.int32)
        itok_B_3_7 = jax.random.randint(jax.random.fold_in(_rk, 11), (64,), 3, 8, jnp.int32)
        itok_B_4_50 = jax.random.randint(jax.random.fold_in(_rk, 12), (64,), 4, 51, jnp.int32)
        return (x, itok_B_3_7, itok_B_4_50)
    x, itok_B_3_7, itok_B_4_50 = _rec_inputs()

    def _L0_cond_setup():
        import jax, jax.numpy as jnp
        import numpy as np
        RANK = 16
        ALPHA = 16.0
        SCALING = ALPHA / RANK
        N_ADAPTERS = 8
        IN_F = 1024
        OUT_F = 1024
        BATCH = 4
        SEQ = 512
        key = jax.random.key(seed)
        kx, ka, kb, ki = jax.random.split(key, 4)
        x = jax.random.normal(kx, (BATCH, SEQ, IN_F), dtype=jnp.float32)
        A = jax.random.normal(ka, (N_ADAPTERS, OUT_F, RANK), dtype=jnp.float32) * 0.02
        B = jax.random.normal(kb, (N_ADAPTERS, RANK, IN_F), dtype=jnp.float32) * 0.02
        adapter_ids = jax.random.randint(ki, (BATCH,), 0, N_ADAPTERS, dtype=jnp.int32)
        return {'x': x, 'A': A, 'B': B, 'adapter_ids': adapter_ids}
    _L0_cond_all = _L0_cond_setup()
    _L0_cond_in = {k: v for k, v in _L0_cond_all.items() if k in ('A', 'B')}
    del _L0_cond_all

    def _L0_ffn_setup():
        import jax, jax.numpy as jnp
        import numpy as np
        SCALING = 16.0 / 8.0
        GAMMA = 1.0
        EPS = 1e-12
        key = jax.random.key(seed)
        ks = jax.random.split(key, 8)
        B, T, H, O = (4, 512, 1024, 1024)
        E_tot, E_act, r = (16, 4, 8)
        return {'x': jax.random.normal(ks[0], (B, T, H), jnp.float32), 'W_base': jax.random.normal(ks[1], (O, H), jnp.float32) * 0.02, 'b_base': jax.random.normal(ks[2], (O,), jnp.float32) * 0.02, 'lora_A': jax.random.normal(ks[3], (E_tot, r, H), jnp.float32) * 0.02, 'lora_B': jax.random.normal(ks[4], (E_tot, O, r), jnp.float32) * 0.02, 'router_W': jax.random.normal(ks[5], (E_tot, H), jnp.float32) * 0.02, 'router_b': jax.random.normal(ks[6], (E_tot,), jnp.float32) * 0.02, 'domain_prior': jax.random.uniform(ks[7], (E_tot,), jnp.float32), 'active': jnp.arange(E_act, dtype=jnp.int32)}
    _L0_ffn_all = _L0_ffn_setup()
    _L0_ffn_in = {k: v for k, v in _L0_ffn_all.items() if k in ('W_base', 'b_base', 'lora_A', 'lora_B', 'router_W', 'router_b', 'domain_prior', 'active')}
    del _L0_ffn_all

    def _L1_cond_setup():
        import jax, jax.numpy as jnp
        import numpy as np
        RANK = 16
        ALPHA = 16.0
        SCALING = ALPHA / RANK
        key = jax.random.key(seed)
        k1, k2, k3, k4 = jax.random.split(key, 4)
        batch, n_tok, d_in, d_out, n_adapters, rank = (8, 512, 1024, 1024, 64, RANK)
        x = jax.random.normal(k1, (batch, n_tok, d_in), dtype=jnp.float32)
        A = jax.random.normal(k2, (n_adapters, d_out, rank), dtype=jnp.float32) * 0.02
        B = jax.random.normal(k3, (n_adapters, rank, d_in), dtype=jnp.float32)
        adapter_ids = jax.random.randint(k4, (batch,), 0, n_adapters, dtype=jnp.int32)
        return {'x': x, 'A': A, 'B': B, 'adapter_ids': adapter_ids}
    _L1_cond_all = _L1_cond_setup()
    _L1_cond_in = {k: v for k, v in _L1_cond_all.items() if k in ('A', 'B')}
    del _L1_cond_all

    def _L1_ffn_setup():
        import jax, jax.numpy as jnp
        import numpy as np
        SCALE = 16.0 / 8.0
        key = jax.random.key(seed)
        ks = jax.random.split(key, 6)
        B, S, IN, OUT, E, R = (4, 512, 1024, 1024, 4, 8)
        x = jax.random.normal(ks[0], (B, S, IN), dtype=jnp.float32)
        W = jax.random.normal(ks[1], (OUT, IN), dtype=jnp.float32) * 0.02
        b = jax.random.normal(ks[2], (OUT,), dtype=jnp.float32) * 0.02
        A = jax.random.normal(ks[3], (E, R, IN), dtype=jnp.float32) * 0.02
        Bm = jax.random.normal(ks[4], (E, OUT, R), dtype=jnp.float32) * 0.02
        Wr = jax.random.normal(ks[5], (E, IN), dtype=jnp.float32) * 0.02
        return {'x': x, 'W': W, 'b': b, 'A': A, 'Bm': Bm, 'Wr': Wr}
    _L1_ffn_all = _L1_ffn_setup()
    _L1_ffn_in = {k: v for k, v in _L1_ffn_all.items() if k in ('W', 'b', 'A', 'Bm', 'Wr')}
    del _L1_ffn_all
    return {'x': x, 'itok_B_3_7': itok_B_3_7, 'itok_B_4_50': itok_B_4_50, 'L0_cond_A': _L0_cond_in['A'], 'L0_cond_B': _L0_cond_in['B'], 'L0_ffn_W_base': _L0_ffn_in['W_base'], 'L0_ffn_b_base': _L0_ffn_in['b_base'], 'L0_ffn_lora_A': _L0_ffn_in['lora_A'], 'L0_ffn_lora_B': _L0_ffn_in['lora_B'], 'L0_ffn_router_W': _L0_ffn_in['router_W'], 'L0_ffn_router_b': _L0_ffn_in['router_b'], 'L0_ffn_domain_prior': _L0_ffn_in['domain_prior'], 'L0_ffn_active': _L0_ffn_in['active'], 'L1_cond_A': _L1_cond_in['A'], 'L1_cond_B': _L1_cond_in['B'], 'L1_ffn_W': _L1_ffn_in['W'], 'L1_ffn_b': _L1_ffn_in['b'], 'L1_ffn_A': _L1_ffn_in['A'], 'L1_ffn_Bm': _L1_ffn_in['Bm'], 'L1_ffn_Wr': _L1_ffn_in['Wr']}

def reference(x, itok_B_3_7, itok_B_4_50, L0_cond_A, L0_cond_B, L0_ffn_W_base, L0_ffn_b_base, L0_ffn_lora_A, L0_ffn_lora_B, L0_ffn_router_W, L0_ffn_router_b, L0_ffn_domain_prior, L0_ffn_active, L1_cond_A, L1_cond_B, L1_ffn_W, L1_ffn_b, L1_ffn_A, L1_ffn_Bm, L1_ffn_Wr):
    import jax
    import jax.numpy as jnp

    def _L0_cond_ref(x, A, B, adapter_ids):
        import jax, jax.numpy as jnp
        import numpy as np
        RANK = 16
        ALPHA = 16.0
        SCALING = ALPHA / RANK
        N_ADAPTERS = 8
        IN_F = 1024
        OUT_F = 1024
        BATCH = 4
        SEQ = 512
        B_sel = B[adapter_ids]
        A_sel = A[adapter_ids]
        Bx = jnp.einsum('bni,bri->bnr', x, B_sel)
        out = jnp.einsum('bnr,bor->bno', Bx, A_sel)
        return out * SCALING

    def _L0_ffn_ref(x, W_base, b_base, lora_A, lora_B, router_W, router_b, domain_prior, active):
        import jax, jax.numpy as jnp
        import numpy as np
        SCALING = 16.0 / 8.0
        GAMMA = 1.0
        EPS = 1e-12
        y = jnp.einsum('bth,oh->bto', x, W_base) + b_base
        A = lora_A[active]
        Bm = lora_B[active]
        z = jnp.einsum('bth,erh->bter', x, A)
        contribs = jnp.einsum('bter,eor->bteo', z, Bm) * SCALING
        logits = jnp.einsum('bth,eh->bte', x, router_W) + router_b
        logits = logits[..., active]
        prior = domain_prior[active]
        alpha = jax.nn.softmax(jnp.log(prior + EPS) + logits / GAMMA, axis=-1)
        return y + jnp.einsum('bteo,bte->bto', contribs, alpha)

    def _L1_cond_ref(x, A, B, adapter_ids):
        import jax, jax.numpy as jnp
        import numpy as np
        RANK = 16
        ALPHA = 16.0
        SCALING = ALPHA / RANK
        B_req = B[adapter_ids]
        A_req = A[adapter_ids]
        Bx = jnp.einsum('bni,bri->bnr', x, B_req)
        out = jnp.einsum('bnr,bor->bno', Bx, A_req)
        return out * SCALING

    def _L1_ffn_ref(x, W, b, A, Bm, Wr):
        import jax, jax.numpy as jnp
        import numpy as np
        SCALE = 16.0 / 8.0
        base_out = jnp.einsum('bsi,oi->bso', x, W) + b
        gates = jax.nn.softmax(jnp.einsum('bsi,ei->bse', x, Wr), axis=-1)
        proj_r = jnp.einsum('bsi,eri->bser', x, A)
        lora_out = jnp.einsum('bser,eor->bseo', proj_r, Bm)
        lora_mix = jnp.einsum('bse,bseo->bso', gates * SCALE, lora_out)
        return base_out + lora_mix
    x = x + _L0_ffn_ref(_L0_cond_ref(x, L0_cond_A, L0_cond_B, itok_B_3_7), L0_ffn_W_base, L0_ffn_b_base, L0_ffn_lora_A, L0_ffn_lora_B, L0_ffn_router_W, L0_ffn_router_b, L0_ffn_domain_prior, L0_ffn_active)
    x = x + _L1_ffn_ref(_L1_cond_ref(x, L1_cond_A, L1_cond_B, itok_B_4_50), L1_ffn_W, L1_ffn_b, L1_ffn_A, L1_ffn_Bm, L1_ffn_Wr)
    return x

_drawn_inputs = setup_inputs


def setup_inputs(seed=0):
    import zlib

    import numpy as np

    out = dict(_drawn_inputs(seed))
    spreads = {}
    factors = {'L0_ffn_b_base': 2.814,
     'L0_ffn_lora_A': 8.0,
     'L0_ffn_lora_B': 8.0,
     'L0_ffn_router_W': 8.0,
     'L0_ffn_router_b': 37.037,
     'L0_ffn_domain_prior': 8.0,
     'L1_ffn_b': 5.347}
    for name, (base, spread) in spreads.items():
        noise = np.random.default_rng([zlib.crc32(name.encode()), seed]).standard_normal(out[name].shape)
        drawn = base * np.exp(spread * noise) if base else spread * noise
        out[name] = jnp.asarray(drawn.astype(out[name].dtype))
    for name, factor in factors.items():
        out[name] = (out[name] * factor).astype(out[name].dtype)
    return out
```

```python
from contextlib import ExitStack

import concourse.bass as bass
from concourse import mybir

F32 = mybir.dt.float32
F32R = mybir.dt.float32r
I32 = mybir.dt.int32
ALU = mybir.AluOpType
ACT = mybir.ActivationFunctionType
AX = mybir.AxisListType

P = 128
D = 1024
KT = D // P
SEQS = 64
LEN = 64
RANK = 16
GROUP = 8
STEPS = SEQS // GROUP
TOK = GROUP * LEN
HALF = TOK // 2
HSEQ = GROUP // 2
HR_ = HSEQ * RANK
ADAPT0 = 8
EXP = 4
ER = 8
LR = EXP * ER
FC = EXP * (ER + 1)
HC = P + LR + 2
CH = 4
KC = KT // CH
TT = TOK // P
SLOT = KT * RANK
WRING = 3
QUARTERS = (2, 3, 0, 1)
EPS = 1e-12

L1ROWS = (slice(0, HR_), slice(HR_, P))
L0ROWS = (slice(HR_, P), slice(0, HR_))
E0ROWS = (slice(HR_, HR_ + LR), slice(0, LR))
E1ROWS = (slice(HR_ + LR, P), slice(LR, 2 * LR))


def two_layer_adapter_lora(nc, x_in, id0_row, id0, id1, act_ids, a0, b0_tab, a1_tab, b1_tab, w0, w1,
                           exp0_in, exp0_rows, exp0_cols, exp0_bias, exp1_in, exp1_rows, bias,
                           consts, out):
    with ExitStack() as ctx:
        def sb(name, shape, dt=F32):
            return ctx.enter_context(nc.sbuf_tensor(name, shape, dt))

        def split(name, shape):
            return sb(name + "_hi", shape, F32R), sb(name + "_lo", shape, F32R)

        def sem(name):
            return ctx.enter_context(nc.semaphore(name))

        def bank(name):
            return ctx.enter_context(nc.psum_tensor(name, [P, 512], F32))

        xraw = [sb(f"xraw{i}", [P, KT, TOK]) for i in range(2)]
        stage = xraw[1][:].rearrange("p k t -> p (k t)").rearrange("p (s n) -> p s n", n=D)
        xs = split("xs", [P, KT, HALF])
        graw = sb("graw", [P, 2 * HSEQ, SLOT])
        bst = split("bst", [P, KT, 4, HR_])
        araw = sb("araw", [P, GROUP, SLOT])
        a1s = split("a1s", [P, KT, GROUP * RANK])
        w1s = split("w1s", [P, KT, D])
        m0s = split("m0s", [P, D])
        hr = split("hr", [P, KT, HC])
        m1x = split("m1x", [P, 2, D])
        k1 = split("k1", [P, TOK])
        k2 = split("k2", [P, TOK])
        c0s = split("c0s", [P, TOK])
        cm = sb("cm", [P, TOK])
        sel = sb("sel", [P, 2, P], F32R)
        hsb = sb("hsb", [P, 2, P])
        hb = hsb[:, 1, LR:LR + 1]
        hts = split("hts", [P, P])
        hls = split("hls", [P, 2, P])
        f0s = split("f0s", [P, FC])
        f1s = split("f1s", [P, 2, FC])
        exp1s = split("exp1s", [P, KT, FC])
        lp = sb("lp", [P, TT * P + HR_])
        lg = sb("lg", [P, TT, EXP])
        mx = sb("mx", [P, TT])
        ex = sb("ex", [P, TT, EXP])
        rs = sb("rs", [P, 2, TT])
        con = sb("con", [P, TOK + 2 * P])
        mask, ident = con[:, 0:TOK], con[:, TOK:TOK + P]
        adapter_of = con[:, TOK + P:TOK + 2 * P]
        idi = sb("idi", [P, 2, STEPS], I32)
        idf = sb("idf", [P, 2, STEPS])
        ids = sb("ids", [1, 2 * SEQS + EXP], I32)
        prb = sb("prb", [P, EXP, 2])
        cb = sb("cb", [P, 2, EXP])
        bia = sb("bia", [P, 2, KT])
        bsum = sb("bsum", [P, KT])

        a0raw = araw[:].rearrange("p b n -> p (b n)")
        m0f = a0raw
        exp0_raw = cm[:, 0:EXP * KT * 9].rearrange("p (e k c) -> p e k c", e=EXP, c=9)
        exp1_raw = lp[:, 0:KT * FC]
        exp0s = tuple(t[:, 0:KT * FC].rearrange("p (k c) -> p k c", c=FC) for t in c0s)
        cols_raw = hsb[:].rearrange("p a n -> p (a n)").rearrange("p (e k r) -> p e k r", e=EXP, r=ER)
        rows_raw = stage[:, WRING, :]
        w0s = tuple(m[:] for m in m1x)

        ps_p, ps_s, ps_z, ps_h, ps_t = (bank(n) for n in ("ps_p", "ps_s", "ps_z", "ps_h", "ps_t"))
        ps_d = [bank(f"ps_d{i}") for i in range(3)]
        z_of = [ps_z[:, i * TT * FC:(i + 1) * TT * FC].rearrange("p (j e c) -> p j e c", j=TT, e=EXP)
                for i in range(2)]
        ps_f = ps_h[:, HC:HC + FC]

        ids_in, id_rows_in, con_in, small_in, a0_in = (
            sem(n) for n in ("ids_in", "id_rows_in", "con_in", "small_in", "a0_in"))
        w_in = [sem(f"w_in{i}") for i in range(WRING)]
        x_in_sem = [sem(f"x_in{i}") for i in range(CH)]
        b_in, a_in = sem("b_in"), sem("a_in")
        stored = [sem(f"stored{i}") for i in range(CH)]
        init_done, pool_init = sem("init_done"), sem("pool_init")
        a0_hi, a0_lo, small_hi, small_lo, rows_hi, rows_lo = (
            sem(n) for n in ("a0_hi", "a0_lo", "small_hi", "small_lo", "rows_hi", "rows_lo"))
        w0_hi, w0_lo, w0_used, w1_hi, w1_lo = (
            sem(n) for n in ("w0_hi", "w0_lo", "w0_used", "w1_hi", "w1_lo"))
        m0_done, m0_hi, m0_copy, m0_lo, m0t_done, m0t_hi, m0t_lo = (
            sem(n) for n in ("m0_done", "m0_hi", "m0_copy", "m0_lo", "m0t_done", "m0t_hi", "m0t_lo"))
        f0_done, f0_hi, f0_lo, bias_step, ln_done = (
            sem(n) for n in ("f0_done", "f0_hi", "f0_lo", "bias_step", "ln_done"))
        x_hi, x_lo, x_used = (sem(n) for n in ("x_hi", "x_lo", "x_used"))
        b_hi, b_lo, a_hi, a_lo = (sem(n) for n in ("b_hi", "b_lo", "a_hi", "a_lo"))
        cm_done, c0_hi, c0_lo, sel_built, sel_done = (
            sem(n) for n in ("cm_done", "c0_hi", "c0_lo", "sel_built", "sel_done"))
        k1_hi, k1_lo, h_done, h_copied, ht_done, ht_hi, ht_lo = (
            sem(n) for n in ("k1_hi", "k1_lo", "h_done", "h_copied", "ht_done", "ht_hi", "ht_lo"))
        m1_done, m1_hi, m1_lo, f1_done, f1_hi, f1_lo = (
            sem(n) for n in ("m1_done", "m1_hi", "m1_lo", "f1_done", "f1_hi", "f1_lo"))
        z_done, sm_step, exp_done, alpha_done, l_done, t_done, l_hi, l_lo = (
            sem(n) for n in ("z_done", "sm_step", "exp_done", "alpha_done", "l_done", "t_done", "l_hi", "l_lo"))
        q_done, qm_done, c1_done, c1_hi, c1_lo = (
            sem(n) for n in ("q_done", "qm_done", "c1_done", "c1_hi", "c1_lo"))
        d_done, d_out = sem("d_done"), sem("d_out")

        block = ctx.enter_context(nc.Block())

        def steps(eng, body, apart=1):
            body(0, 0, False)
            with eng.Fori(0, (STEPS - 1 - apart) // 2) as turn:
                for u in range(2):
                    body(2 * turn + (u + 1), (u + 1) % 2, False)
            for g in range(STEPS - apart, STEPS):
                body(g, g % 2, g == STEPS - 1)

        def after_step(eng, signal, count):
            if not (isinstance(count, int) and count == 0):
                eng.wait_ge(signal, count)

        @block.sync
        def _(sp):
            def load_x(g, par, i):
                sp.dma_start(xraw[par][:, KC * i:KC * (i + 1), :],
                             x_in[bass.ds(g, 1), :, KC * i:KC * (i + 1), :]
                             .rearrange("a p k t -> p (a k) t")).then_inc(x_in_sem[i], 16)

            def adapter(g, b, layer):
                return sp.value_load(ids[0:1, bass.ds(g * GROUP + (layer * SEQS + b), 1)],
                                     min_val=0, max_val=(SEQS if layer else ADAPT0) - 1)

            def gather_b(g, half, free):
                picks = [(b, layer, adapter(g, b, layer))
                         for b in range(half * HSEQ, (half + 1) * HSEQ) for layer in range(2)]
                after_step(sp, b_lo, free)
                for b, layer, n in picks:
                    place = half if layer else 1 - half
                    sp.dma_start(graw[:, place * HSEQ + b % HSEQ, :],
                                 (b1_tab if layer else b0_tab)[bass.ds(n, 1)]
                                 .rearrange("a p n -> p (a n)")).then_inc(b_in, 16)

            def gather_a(g):
                picks = [adapter(g, b, 1) for b in range(GROUP)]
                after_step(sp, a_lo, g)
                for b, n in enumerate(picks):
                    sp.dma_start(araw[:, b, :],
                                 a1_tab[bass.ds(n, 1)].rearrange("a p n -> p (a n)")).then_inc(a_in, 16)

            sp.dma_start(ids[0:1, 0:SEQS], id0).then_inc(ids_in, 16)
            sp.dma_start(ids[0:1, SEQS:2 * SEQS], id1).then_inc(ids_in, 16)
            sp.dma_start(ids[0:1, 2 * SEQS:], act_ids).then_inc(ids_in, 16)
            sp.wait_ge(ids_in, 48)
            gather_b(0, 0, 0)
            for i in range(CH):
                load_x(0, 0, i)
            gather_b(0, 1, 2)
            sp.dma_start(con[:], consts).then_inc(con_in, 16)
            for half in range(2):
                sp.dma_start(idi[L0ROWS[half], half, :], id0_row[half]).then_inc(id_rows_in, 16)
            sp.dma_start(a0raw, a0).then_inc(a0_in, 16)
            for e in range(EXP):
                n = sp.value_load(ids[0:1, 2 * SEQS + e:2 * SEQS + e + 1], min_val=0, max_val=15)
                sp.dma_start(exp0_raw[:, e], exp0_in[bass.ds(n, 1)].rearrange("a p k c -> p (a k) c")
                             ).then_inc(small_in, 16)
                sp.dma_start(cols_raw[:, e], exp0_cols[bass.ds(n, 1)].rearrange("a p k r -> p (a k) r")
                             ).then_inc(small_in, 16)
                sp.dma_start(prb[:, e, :], exp0_bias[bass.ds(n, 1)].rearrange("a p c -> p (a c)")
                             ).then_inc(small_in, 16)
                for half in range(2):
                    r0 = E0ROWS[half].start + e * ER
                    sp.dma_start(rows_raw[r0:r0 + ER, :],
                                 exp0_rows[bass.ds(n, 1)].rearrange("a r o -> (a r) o")).then_inc(small_in, 16)
            for half in range(2):
                sp.dma_start(rows_raw[E1ROWS[half], :], exp1_rows).then_inc(small_in, 16)
            sp.dma_start(exp1_raw, exp1_in).then_inc(small_in, 16)
            sp.dma_start(bia[:], bias).then_inc(small_in, 16)
            for k in range(2 * KT):
                if k >= WRING:
                    j = k - WRING
                    sp.wait_ge(w0_lo if j < KT else w1_lo, j % KT + 1)
                w = w0 if k < KT else w1
                sp.dma_start(stage[:, k % WRING, :], w[k % KT]).then_inc(w_in[k % WRING], 16)
            sp.wait_ge(m0t_done, 1)
            gather_a(0)
            sp.wait_ge(w1_lo, KT)
            sp.wait_ge(rows_lo, 1)
            for i in range(CH):
                load_x(1, 1, i)

            gather_b(1, 0, 4)

            def body(g, par, last):
                if not last:
                    gather_a(g + 1)
                    gather_b(g + 1, 1, 4 * g + 6)
                if not (isinstance(g, int) and g >= STEPS - 2):
                    gather_b(g + 2, 0, 4 * g + 8)
                for i in range(CH):
                    sp.wait_ge(d_out, KT * g + KC * (i + 1))
                    sp.dma_start(out[bass.ds(g, 1), :, KC * i:KC * (i + 1), :]
                                 .rearrange("a p k t -> p (a k) t"),
                                 xraw[par][:, KC * i:KC * (i + 1), :]).then_inc(stored[i], 16)
                    if i and not (isinstance(g, int) and g >= STEPS - 2):
                        sp.wait_ge(stored[i - 1], 16 * g + 16)
                        load_x(g + 2, par, i - 1)
                if not (isinstance(g, int) and g >= STEPS - 2):
                    sp.wait_ge(stored[CH - 1], 16 * g + 16)
                    load_x(g + 2, par, CH - 1)

            steps(sp, body, 3)
            for i in range(CH):
                sp.wait_ge(stored[i], 16 * STEPS)

        @block.tensor
        def _(pe):
            def product(acc, left, right, first=True, final=True):
                (lh, ll), (rh, rl) = left, right
                pe.matmul(acc, lh, rh, start=first, stop=False, skip_group_check=True)
                pe.matmul(acc, lh, rl, start=False, stop=False, skip_group_check=True)
                return pe.matmul(acc, ll, rh, start=False, stop=final, skip_group_check=True)

            def part(pair, *index):
                return tuple(t[index] for t in pair)

            ALL = slice(None)

            def project(g, half):
                n = 2 * g + half
                if half == 0:
                    pe.wait_ge(b_lo, 4 * g + 4)
                    after_step(pe, cm_done, g)
                for kc in range(CH):
                    pe.wait_ge(x_lo, CH * n + kc + 1)
                    for k in range(KC * kc, KC * (kc + 1)):
                        cols = tuple(t[:, k, 2 - 2 * half:4 - 2 * half, :].rearrange("p a n -> p (a n)")
                                     for t in bst)
                        mm = product(ps_p[:, half * HALF:(half + 1) * HALF], cols, part(xs, ALL, k, ALL),
                                     k == 0, k == KT - 1)
                    mm.then_inc(x_used, 1)

            project(0, 0)
            project(0, 1)
            pe.wait_ge(a0_lo, 1)
            for k in range(KT):
                pe.wait_ge(w0_lo, k + 1)
                for h in range(2):
                    mm = product(ps_d[h][:], part(a1s, ALL, k, ALL),
                                 tuple(w[:, k % 2, h * 512:(h + 1) * 512] for w in w0s), k == 0, k == KT - 1)
                mm.then_inc(w0_used, 1)
            pe.wait_ge(small_lo, 4)
            for k in range(KT):
                mm = product(ps_z[:, 0:FC], part(a1s, ALL, k, ALL), part(exp0s, ALL, k, ALL),
                             k == 0, k == KT - 1)
            mm.then_inc(f0_done, 1)
            pe.wait_ge(m0_copy, 2)
            pe.wait_ge(con_in, 16)
            for k in range(KT):
                to = ps_d[2] if k < KT // 2 else ps_t
                mm = pe.transpose(to[:, (k % 4) * P:(k % 4 + 1) * P], m0f[:, k * P:(k + 1) * P], ident)
            mm.then_inc(m0t_done, 1)
            pe.wait_ge(m0t_lo, 2)
            pe.wait_ge(init_done, 3)
            pe.wait_ge(pool_init, 1)

            def body(g, par, last):
                after_step(pe, f1_lo, 2 * g)
                for k in range(KT):
                    rows = tuple(t[:, k, 1:3, :].rearrange("p a n -> p (a n)") for t in bst)
                    mm = product(ps_h[:, 0:HC], rows, part(hr, ALL, k, ALL), k == 0, k == KT - 1)
                mm.then_inc(h_done, 1)
                pe.wait_ge(sel_built, 2 * g + 2)
                pe.wait_ge(c0_lo, g + 1)
                after_step(pe, c1_done, g)
                for half in range(2):
                    cols = slice(half * HALF, (half + 1) * HALF)
                    pe.matmul(ps_s[:, cols], sel[:, half, :], c0s[0][:, cols], start=True, stop=False,
                              skip_group_check=True)
                    mm = pe.matmul(ps_s[:, cols], sel[:, half, :], c0s[1][:, cols], start=False, stop=True,
                                   skip_group_check=True)
                mm.then_inc(sel_done, 1)

                def wide(h):
                    for k in range(KT):
                        mm = product(ps_d[h][:], part(a1s, ALL, k, ALL),
                                     part(w1s, ALL, k, slice(h * 512, (h + 1) * 512)), k == 0, k == KT - 1)
                    mm.then_inc(m1_done, 1)

                def route(layer, coefs, weights):
                    for j in range(TT):
                        w = part(weights, ALL, j // 2, ALL) if layer else part(weights, ALL, ALL)
                        at = layer * TT * FC + j * FC
                        mm = product(ps_z[:, at:at + FC], part(coefs, ALL, slice(j * P, (j + 1) * P)), w)
                    mm.then_inc(z_done, 1)

                def turn():
                    for j in range(TT):
                        at = j * P + (j // 2) * HR_
                        mm = pe.transpose(ps_t[:, j * P:(j + 1) * P], lp[:, at:at + P], ident)
                    mm.then_inc(t_done, 1)

                pe.wait_ge(a_lo, g + 1)
                if isinstance(g, int) and g == 0:
                    pe.wait_ge(w1_lo, KT)
                after_step(pe, d_out, KT * g)
                wide(0)
                pe.wait_ge(h_copied, 2 * g + 2)
                after_step(pe, l_lo, 4 * g)
                pe.transpose(ps_t[:, 0:P], hsb[:, 0, :], ident)
                pe.transpose(ps_t[:, P:2 * P], hsb[:, 1, :], ident).then_inc(ht_done, 1)
                pe.wait_ge(k1_lo, g + 1)
                pe.wait_ge(f0_lo, 1)
                after_step(pe, l_done, 2 * g)
                route(0, k1, f0s)
                wide(1)
                pe.wait_ge(l_done, 2 * g + 1)
                pe.wait_ge(ht_lo, g + 1)
                turn()
                product(ps_s[:], part(hts, ALL, ALL), part(k1, ALL, ALL), True, False)
                for k in range(KT):
                    mm = product(ps_f, part(a1s, ALL, k, ALL), part(exp1s, ALL, k, ALL), k == 0, k == KT - 1)
                mm.then_inc(f1_done, 1)
                pe.wait_ge(l_lo, 4 * g + 2)
                for half in range(2):
                    cols = slice(half * HALF, (half + 1) * HALF)
                    mm = product(ps_s[:, cols], part(hls, ALL, half, ALL), part(k2, ALL, cols), False, True)
                mm.then_inc(q_done, 1)
                if not last:
                    project(g + 1, 0)
                pe.wait_ge(c1_lo, 2 * g + 2)
                pe.wait_ge(f1_lo, 2 * g + 2)
                route(1, k2, f1s)
                if not last:
                    project(g + 1, 1)
                pe.wait_ge(l_done, 2 * g + 2)
                turn()

                def from_layer0(m):
                    product(ps_d[m % 3][:], part(m0s, ALL, slice(m * P, (m + 1) * P)), part(k1, ALL, ALL),
                            True, False)

                pe.wait_ge(m1_lo, 4 * g + 4)
                for m in range(3):
                    from_layer0(m)
                pe.wait_ge(l_lo, 4 * g + 4)
                for m in range(KT):
                    if m >= 3:
                        pe.wait_ge(d_out, KT * g + m - 2)
                        from_layer0(m)
                    for half in range(2):
                        cols = slice(half * HALF, (half + 1) * HALF)
                        mm = product(ps_d[m % 3][:, cols], part(m1x, ALL, half, slice(m * P, (m + 1) * P)),
                                     part(k2, ALL, cols), False, True)
                    mm.then_inc(d_done, 1)

            steps(pe, body)

        @block.scalar
        def _(act):
            def copy(dst, src):
                return act.activation(dst, src, ACT.Copy)

            def split_x(g, par, half):
                n = 2 * g + half
                for i in range(CH):
                    act.wait_ge(x_in_sem[i], 16 * g + 16)
                    if not (isinstance(n, int) and n == 0):
                        act.wait_ge(x_used, CH * n + (i + 1 - CH))
                    copy(xs[0][:, KC * i:KC * (i + 1), :],
                         xraw[par][:, KC * i:KC * (i + 1), half * HALF:(half + 1) * HALF]).then_inc(x_hi, 1)

            def split_b(g):
                for n, q in enumerate(QUARTERS):
                    if n % 2 == 0:
                        act.wait_ge(b_in, 16 * GROUP * (2 * g + n // 2 + 1))
                    copy(bst[0][:, :, q, :].rearrange("p k (b r) -> p b k r", b=HSEQ),
                         graw[:, q % 2 * HSEQ:(q % 2 + 1) * HSEQ, :].rearrange("p b (k r) -> p b k r", k=KT)
                         ).then_inc(b_hi, 1)

            def split_a(g):
                act.wait_ge(a_in, 16 * GROUP * (g + 1))
                copy(a1s[0][:].rearrange("p k (b r) -> p b k r", b=GROUP),
                     araw[:].rearrange("p b (k r) -> p b k r", k=KT)).then_inc(a_hi, 1)

            def c0_high(g):
                act.wait_ge(cm_done, g + 1)
                copy(c0s[0][:], cm[:]).then_inc(c0_hi, 1)

            split_b(0)
            split_x(0, 0, 0)
            act.wait_ge(a0_in, 16)
            copy(a1s[0][:].rearrange("p k n -> p (k n)"), a0raw).then_inc(a0_hi, 1)
            split_x(0, 0, 1)
            act.wait_ge(small_in, 16 * (5 * EXP + 4))
            copy(exp0s[0].rearrange("p k (e c) -> p e k c", e=EXP), exp0_raw).then_inc(small_hi, 1)
            copy(exp1s[0][:].rearrange("p k c -> p (k c)"), exp1_raw).then_inc(small_hi, 1)
            act.wait_ge(init_done, 1)
            copy(hr[0][:, :, P:P + LR].rearrange("p k (e r) -> p e k r", e=EXP), cols_raw).then_inc(small_hi, 1)
            copy(hr[0][:, :, P + LR:P + LR + 1], bia[:, 0, :].rearrange("p (k a) -> p k a", a=1)
                 ).then_inc(small_hi, 1)
            for k in range(KT):
                act.wait_ge(w_in[k % WRING], 16 * (k // WRING + 1))
                if k >= 2:
                    act.wait_ge(w0_used, k - 1)
                copy(w0s[0][:, k % 2, :], stage[:, k % WRING, :]).then_inc(w0_hi, 1)
            for h in range(2):
                if h == 0:
                    act.wait_ge(w0_used, KT)
                    act.wait_ge(a0_lo, 1)
                copy(m0s[0][:, h * 512:(h + 1) * 512], ps_d[h][:]).then_inc(m0_hi, 1)
                copy(m0f[:, h * 512:(h + 1) * 512], ps_d[h][:]).then_inc(m0_copy, 1)
            for half in range(2):
                copy(m1x[0][L0ROWS[half], half, :], rows_raw[L0ROWS[half], :]).then_inc(rows_hi, 1)
            act.wait_ge(f0_done, 1)
            copy(f0s[0][:], ps_z[:, 0:FC]).then_inc(f0_hi, 1)
            act.wait_ge(m0t_done, 1)
            for h, src in enumerate((ps_d[2], ps_t)):
                copy(hr[0][:, 4 * h:4 * h + 4, 0:P], src[:].rearrange("p (k n) -> p k n", n=P)
                     ).then_inc(m0t_hi, 1)
            act.wait_ge(bias_step, 2)
            act.activation(cb[:, 1, :], cb[:, 0, :], ACT.Ln).then_inc(ln_done, 1)
            c0_high(0)
            for k in range(KT):
                n = KT + k
                act.wait_ge(w_in[n % WRING], 16 * (n // WRING + 1))
                copy(w1s[0][:, k, :], stage[:, n % WRING, :]).then_inc(w1_hi, 1)
            split_a(0)
            act.wait_ge(pool_init, 1)

            def body(g, par, last):
                act.wait_ge(h_done, g + 1)
                after_step(act, qm_done, g)
                whole = hsb[:].rearrange("p a n -> p (a n)")
                for half in range(2):
                    to, rows = L1ROWS[half], L1ROWS[1 - half]
                    copy(whole[to, 0:HC], ps_h[rows, 0:HC])
                    copy(whole[to, P + HR_:P + HR_ + LR], ps_h[rows, P:P + LR]).then_inc(h_copied, 1)
                act.wait_ge(sel_done, g + 1)
                copy(k1[0][:], ps_s[:]).then_inc(k1_hi, 1)
                if not last:
                    split_b(g + 1)
                act.wait_ge(m1_done, 2 * g + 1)

                def wide_high(h):
                    for half in range(2):
                        copy(m1x[0][L1ROWS[half], half, h * 512:(h + 1) * 512],
                             ps_d[h][L1ROWS[half], :]).then_inc(m1_hi, 1)

                def coef_high(layer):
                    act.wait_ge(t_done, 2 * g + layer + 1)
                    for half in range(2):
                        rows, cols = (E0ROWS, E1ROWS)[layer][half], slice(half * HALF, (half + 1) * HALF)
                        copy(k2[0][rows, cols], ps_t[rows, cols]).then_inc(l_hi, 1)

                def softmax_exp(layer):
                    act.wait_ge(sm_step, 10 * g + 5 * layer + 3)
                    act.activation(ex[:], lg[:], ACT.Exp).then_inc(exp_done, 1)

                wide_high(0)
                act.wait_ge(ht_done, g + 1)
                copy(hts[0][:], ps_t[:, 0:P]).then_inc(ht_hi, 1)
                for half in range(2):
                    rows = E0ROWS[half]
                    copy(hls[0][rows, half, :], ps_t[rows, P:2 * P]).then_inc(ht_hi, 1)
                softmax_exp(0)
                if not last:
                    split_x(g + 1, 1 - par, 0)
                coef_high(0)
                act.wait_ge(m1_done, 2 * g + 2)
                wide_high(1)
                act.wait_ge(f1_done, g + 1)
                for half in range(2):
                    copy(f1s[0][L1ROWS[half], half, :], ps_f[L1ROWS[half], :]).then_inc(f1_hi, 1)
                act.wait_ge(c1_done, g + 1)
                for half in range(2):
                    cols = slice(half * HALF, (half + 1) * HALF)
                    copy(k2[0][L1ROWS[half], cols], cm[L1ROWS[half], cols]).then_inc(c1_hi, 1)
                if not last:
                    split_x(g + 1, 1 - par, 1)
                softmax_exp(1)
                if not last:
                    split_a(g + 1)
                coef_high(1)
                if not last:
                    c0_high(g + 1)

            steps(act, body)

        @block.vector
        def _(dve):
            def low(dst, whole, high):
                return dve.tensor_tensor(dst, whole, high.bitcast(F32), ALU.subtract)

            def masked(g):
                dve.wait_ge(x_used, 2 * CH * (g + 1))
                dve.tensor_tensor(cm[:], ps_p[:], mask, ALU.mult).then_inc(cm_done, 1)
                after_step(dve, sel_done, g)
                for half in range(2):
                    dve.tensor_scalar(sel[:, half, :], adapter_of, idf[:, half, bass.ds(g, 1)], None,
                                      ALU.is_equal).then_inc(sel_built, 1)
                dve.wait_ge(c0_hi, g + 1)
                low(c0s[1][:], cm[:], c0s[0][:]).then_inc(c0_lo, 1)

            for t in (*hls, *f1s, *k2):
                dve.memset(t[:].bitcast(F32), 0.0)
            for t in hr:
                dve.memset(t[:, :, HC - 1:HC].bitcast(F32), 0.0)
            dve.memset(idf[:], -1.0).then_inc(init_done, 1)
            dve.wait_ge(init_done, 1)
            dve.wait_ge(id_rows_in, 32)
            for half in range(2):
                ins = dve.tensor_copy(idf[L0ROWS[half], half, :], idi[L0ROWS[half], half, :])
            ins.then_inc(init_done, 1)
            dve.wait_ge(a0_hi, 1)
            low(a1s[1][:].rearrange("p k n -> p (k n)"), a0raw, a1s[0][:].rearrange("p k n -> p (k n)")
                ).then_inc(a0_lo, 1)
            dve.wait_ge(small_hi, 4)
            low(exp0s[1].rearrange("p k (e c) -> p e k c", e=EXP), exp0_raw,
                exp0s[0].rearrange("p k (e c) -> p e k c", e=EXP)).then_inc(small_lo, 1)
            low(exp1s[1][:].rearrange("p k c -> p (k c)"), exp1_raw,
                exp1s[0][:].rearrange("p k c -> p (k c)")).then_inc(small_lo, 1)
            low(hr[1][:, :, P:P + LR].rearrange("p k (e r) -> p e k r", e=EXP), cols_raw,
                hr[0][:, :, P:P + LR].rearrange("p k (e r) -> p e k r", e=EXP)).then_inc(small_lo, 1)
            low(hr[1][:, :, P + LR:P + LR + 1], bia[:, 0, :].rearrange("p (k a) -> p k a", a=1),
                hr[0][:, :, P + LR:P + LR + 1]).then_inc(small_lo, 1)
            dve.wait_ge(small_lo, 2)
            dve.memset(lp[:], 0.0).then_inc(init_done, 1)
            dve.tensor_tensor(bsum[:], bia[:, 0, :], bia[:, 1, :], ALU.add).then_inc(bias_step, 1)
            dve.tensor_scalar(cb[:, 0, :], prb[:, :, 1], EPS, None, ALU.add).then_inc(bias_step, 1)
            for k in range(KT):
                dve.wait_ge(w0_hi, k + 1)
                low(w0s[1][:, k % 2, :], stage[:, k % WRING, :], w0s[0][:, k % 2, :]).then_inc(w0_lo, 1)
            for h in range(2):
                dve.wait_ge(m0_copy, h + 1)
                low(m0s[1][:, h * 512:(h + 1) * 512], ps_d[h][:], m0s[0][:, h * 512:(h + 1) * 512]
                    ).then_inc(m0_lo, 1)
            dve.wait_ge(rows_hi, 2)
            for half in range(2):
                ins = low(m1x[1][L0ROWS[half], half, :], rows_raw[L0ROWS[half], :], m1x[0][L0ROWS[half], half, :])
            ins.then_inc(rows_lo, 1)
            dve.wait_ge(f0_hi, 1)
            low(f0s[1][:], ps_z[:, 0:FC], f0s[0][:]).then_inc(f0_lo, 1)
            for h, src in enumerate((ps_d[2], ps_t)):
                dve.wait_ge(m0t_hi, h + 1)
                low(hr[1][:, 4 * h:4 * h + 4, 0:P], src[:].rearrange("p (k n) -> p k n", n=P),
                    hr[0][:, 4 * h:4 * h + 4, 0:P]).then_inc(m0t_lo, 1)
            dve.wait_ge(ln_done, 1)
            dve.tensor_tensor(cb[:, 0, :], cb[:, 1, :], prb[:, :, 0], ALU.add).then_inc(bias_step, 1)
            dve.wait_ge(con_in, 16)
            dve.wait_ge(init_done, 3)
            dve.wait_ge(bias_step, 3)
            masked(0)

            def body(g, par, last):
                dve.wait_ge(k1_hi, g + 1)
                low(k1[1][:], ps_s[:], k1[0][:]).then_inc(k1_lo, 1)

                def wide_low(h):
                    for half in range(2):
                        dve.wait_ge(m1_hi, 4 * g + 2 * h + half + 1)
                        low(m1x[1][L1ROWS[half], half, h * 512:(h + 1) * 512], ps_d[h][L1ROWS[half], :],
                            m1x[0][L1ROWS[half], half, h * 512:(h + 1) * 512]).then_inc(m1_lo, 1)

                def coef_low(layer):
                    for half in range(2):
                        rows, cols = (E0ROWS, E1ROWS)[layer][half], slice(half * HALF, (half + 1) * HALF)
                        dve.wait_ge(l_hi, 4 * g + 2 * layer + half + 1)
                        low(k2[1][rows, cols], ps_t[rows, cols], k2[0][rows, cols]).then_inc(l_lo, 1)

                def softmax(layer):
                    z = z_of[layer]
                    at = 10 * g + 5 * layer
                    dve.wait_ge(z_done, 2 * g + layer + 1)
                    if layer == 0:
                        dve.tensor_tensor(lg[:], z[:, :, :, ER],
                                          cb[:, 0:1, :].to_broadcast([P, TT, EXP]), ALU.add).then_inc(sm_step, 1)
                    else:
                        dve.tensor_copy(lg[:], z[:, :, :, ER]).then_inc(sm_step, 1)
                    dve.wait_ge(sm_step, at + 1)
                    dve.tensor_reduce(mx[:], lg[:], AX.X, ALU.max).then_inc(sm_step, 1)
                    dve.wait_ge(sm_step, at + 2)
                    dve.tensor_tensor(lg[:], lg[:],
                                      mx[:].rearrange("p (j a) -> p j a", a=1).to_broadcast([P, TT, EXP]),
                                      ALU.subtract).then_inc(sm_step, 1)
                    dve.wait_ge(exp_done, 2 * g + layer + 1)
                    dve.tensor_reduce(rs[:, 0, :], ex[:], AX.X, ALU.add).then_inc(sm_step, 1)
                    dve.wait_ge(sm_step, at + 4)
                    dve.reciprocal(rs[:, 1, :], rs[:, 0, :]).then_inc(sm_step, 1)
                    dve.wait_ge(sm_step, at + 5)
                    dve.scalar_tensor_tensor(out=lg[:], in0=ex[:], scalar=2.0,
                                             in1=rs[:, 1, :].rearrange("p (j a) -> p j a", a=1)
                                             .to_broadcast([P, TT, EXP]),
                                             op0=ALU.mult, op1=ALU.mult).then_inc(alpha_done, 1)
                    dve.wait_ge(alpha_done, 2 * g + layer + 1)
                    to = lp[:, HR_:HR_ + TT * P].rearrange("p (j e r) -> p j e r", j=TT, r=ER)[
                        :, :, layer * EXP:(layer + 1) * EXP, :]
                    dve.tensor_tensor(to, z[:, :, :, 0:ER],
                                      lg[:].rearrange("p j (e a) -> p j e a", a=1)
                                      .to_broadcast([P, TT, EXP, ER]), ALU.mult).then_inc(l_done, 1)

                wide_low(0)
                dve.wait_ge(ht_hi, 3 * g + 3)
                low(hts[1][:], ps_t[:, 0:P], hts[0][:])
                for half in range(2):
                    rows = E0ROWS[half]
                    ins = low(hls[1][rows, half, :], ps_t[rows, P:2 * P], hls[0][rows, half, :])
                ins.then_inc(ht_lo, 1)
                softmax(0)
                coef_low(0)
                for half in range(2):
                    dve.wait_ge(f1_hi, 2 * g + half + 1)
                    low(f1s[1][L1ROWS[half], half, :], ps_f[L1ROWS[half], :], f1s[0][L1ROWS[half], half, :]
                        ).then_inc(f1_lo, 1)
                dve.wait_ge(q_done, g + 1)
                dve.wait_ge(h_copied, 2 * g + 2)
                dve.scalar_tensor_tensor(out=ps_s[:], in0=ps_s[:], scalar=hb, in1=mask,
                                         op0=ALU.add, op1=ALU.mult).then_inc(qm_done, 1)
                dve.wait_ge(qm_done, g + 1)
                dve.tensor_tensor(cm[:], cm[:], ps_s[:], ALU.add).then_inc(c1_done, 1)
                for half in range(2):
                    cols = slice(half * HALF, (half + 1) * HALF)
                    dve.wait_ge(c1_hi, 2 * g + half + 1)
                    low(k2[1][L1ROWS[half], cols], cm[L1ROWS[half], cols], k2[0][L1ROWS[half], cols]
                        ).then_inc(c1_lo, 1)
                wide_low(1)
                softmax(1)
                coef_low(1)
                if not last:
                    masked(g + 1)
                for m in range(KT):
                    dve.wait_ge(d_done, KT * g + m + 1)
                    dve.scalar_tensor_tensor(out=xraw[par][:, m, :], in0=ps_d[m % 3][:],
                                             scalar=bsum[:, m:m + 1], in1=xraw[par][:, m, :],
                                             op0=ALU.add, op1=ALU.add).then_inc(d_out, 1)

            steps(dve, body)

        @block.gpsimd
        def _(pool):
            def low(dst, whole, high):
                return pool.tensor_tensor(dst, whole, high.bitcast(F32), ALU.subtract)

            def split_x(g, par, half):
                n = 2 * g + half
                for i in range(CH):
                    pool.wait_ge(x_hi, CH * n + i + 1)
                    low(xs[1][:, KC * i:KC * (i + 1), :],
                        xraw[par][:, KC * i:KC * (i + 1), half * HALF:(half + 1) * HALF],
                        xs[0][:, KC * i:KC * (i + 1), :]).then_inc(x_lo, 1)

            def split_b(g):
                for n, q in enumerate(QUARTERS):
                    pool.wait_ge(b_hi, 4 * g + n + 1)
                    low(bst[1][:, :, q, :].rearrange("p k (b r) -> p b k r", b=HSEQ),
                        graw[:, q % 2 * HSEQ:(q % 2 + 1) * HSEQ, :].rearrange("p b (k r) -> p b k r", k=KT),
                        bst[0][:, :, q, :].rearrange("p k (b r) -> p b k r", b=HSEQ)).then_inc(b_lo, 1)

            def split_a(g):
                pool.wait_ge(a_hi, g + 1)
                low(a1s[1][:].rearrange("p k (b r) -> p b k r", b=GROUP),
                    araw[:].rearrange("p b (k r) -> p b k r", k=KT),
                    a1s[0][:].rearrange("p k (b r) -> p b k r", b=GROUP)).then_inc(a_lo, 1)

            split_b(0)
            split_x(0, 0, 0)
            split_x(0, 0, 1)
            pool.wait_ge(small_lo, 4)
            pool.memset(hsb[:, 1, :], 0.0).then_inc(pool_init, 1)
            for k in range(KT):
                pool.wait_ge(w1_hi, k + 1)
                low(w1s[1][:, k, :], stage[:, (KT + k) % WRING, :], w1s[0][:, k, :]).then_inc(w1_lo, 1)
            split_a(0)

            def body(g, par, last):
                if not last:
                    split_b(g + 1)
                    split_x(g + 1, 1 - par, 0)
                    split_x(g + 1, 1 - par, 1)
                    split_a(g + 1)

            steps(pool, body)


def kernel(x, itok_B_3_7, itok_B_4_50, L0_cond_A, L0_cond_B, L0_ffn_W_base, L0_ffn_b_base, L0_ffn_lora_A,
           L0_ffn_lora_B, L0_ffn_router_W, L0_ffn_router_b, L0_ffn_domain_prior, L0_ffn_active, L1_cond_A,
           L1_cond_B, L1_ffn_W, L1_ffn_b, L1_ffn_A, L1_ffn_Bm, L1_ffn_Wr):
    import numpy as np
    import concourse.bacc as bacc
    from concourse.bass_utils import run_bass_kernel_spmd

    x, id0, id1, A0, B0, W0, b0, EA, EB, RW, Rb, prior, active, A1, B1, W1, b1, LA, LB, WR = (
        np.asarray(a) for a in (
            x, itok_B_3_7, itok_B_4_50, L0_cond_A, L0_cond_B, L0_ffn_W_base, L0_ffn_b_base, L0_ffn_lora_A,
            L0_ffn_lora_B, L0_ffn_router_W, L0_ffn_router_b, L0_ffn_domain_prior, L0_ffn_active, L1_cond_A,
            L1_cond_B, L1_ffn_W, L1_ffn_b, L1_ffn_A, L1_ffn_Bm, L1_ffn_Wr))

    def tiles(a):
        return np.swapaxes(a.reshape(*a.shape[:-1], KT, P), -1, -2)

    n_exp = EA.shape[0]
    rows = np.arange(P)
    seq_of_row, seq_of_col = rows % HR_ // RANK, np.arange(TOK) // LEN % HSEQ
    consts = np.concatenate([
        seq_of_row[:, None] == seq_of_col[None, :],
        np.eye(P),
        np.where(rows[:, None] % RANK == rows[None, :] % RANK, rows[None, :] // RANK, -2),
    ], axis=1).astype(np.float32)
    named = {
        "x_in": x.reshape(STEPS, TOK, KT, P).transpose(0, 3, 2, 1),
        "id0_row": np.repeat(id0.reshape(STEPS, 2, HSEQ).transpose(1, 2, 0), RANK, axis=1),
        "id0": id0.reshape(1, -1),
        "id1": id1.reshape(1, -1),
        "act_ids": active.reshape(1, -1),
        "a0": tiles(A0.transpose(0, 2, 1)).transpose(2, 3, 0, 1).reshape(P, -1),
        "b0_tab": tiles(B0).transpose(0, 2, 3, 1).reshape(ADAPT0, P, -1),
        "a1_tab": A1.reshape(SEQS, KT, P, RANK).transpose(0, 2, 1, 3).reshape(SEQS, P, -1),
        "b1_tab": tiles(B1).transpose(0, 2, 3, 1).reshape(SEQS, P, -1),
        "w0": W0.T.reshape(KT, P, D),
        "w1": W1.T.reshape(KT, P, D),
        "exp0_in": tiles(np.concatenate([EA, RW[:, None, :]], axis=1)).transpose(0, 2, 3, 1),
        "exp0_rows": EB.transpose(0, 2, 1),
        "exp0_cols": EB.reshape(n_exp, KT, P, ER).transpose(0, 2, 1, 3),
        "exp0_bias": np.repeat(np.stack([Rb, prior], axis=1)[:, None, :], P, axis=1),
        "exp1_in": tiles(np.concatenate([LA, WR[:, None, :]], axis=1)).transpose(2, 3, 0, 1).reshape(P, -1),
        "exp1_rows": LB.transpose(0, 2, 1).reshape(LR, D),
        "bias": tiles(np.stack([b0, b1])).transpose(1, 0, 2),
        "consts": consts,
    }
    nc = bacc.Bacc("TRN2", target_bir_lowering=False, num_devices=1)
    arrays, args = {}, []
    for name, a in named.items():
        a = np.ascontiguousarray(a)
        arrays[name] = a
        args.append(nc.dram_tensor(name, a.shape, mybir.dt.from_np(a.dtype), kind="ExternalInput").ap())
    out = nc.dram_tensor("out", (STEPS, P, KT, TOK), F32, kind="ExternalOutput").ap()
    two_layer_adapter_lora(nc, *args, out)
    r = run_bass_kernel_spmd(nc, [arrays], core_ids=[0])
    y = r.results[0]["out"].reshape(STEPS, P, KT, TOK)
    return y.transpose(0, 3, 2, 1).reshape(SEQS, LEN, D)
```

```python
from contextlib import ExitStack

import concourse.bass as bass
from concourse import mybir

F32 = mybir.dt.float32
F32R = mybir.dt.float32r
BF16 = mybir.dt.bfloat16
I32 = mybir.dt.int32
ALU = mybir.AluOpType
ACT = mybir.ActivationFunctionType
AX = mybir.AxisListType

P = 128
D = 1024
KT = D // P
SEQS = 64
LEN = 64
RANK = 16
GROUP = 8
STEPS = SEQS // GROUP
TOK = GROUP * LEN
HALF = TOK // 2
HSEQ = GROUP // 2
HR_ = HSEQ * RANK
ADAPT0 = 8
EXP = 4
ER = 8
LR = EXP * ER
FC = EXP * (ER + 1)
HC = P + LR + 2
CH = 4
KC = KT // CH
TT = TOK // P
SLOT = KT * RANK
PACK = KT * (2 * ER + 1) + 2
SLOTS = 2 * CH
SPARE = SLOTS - 1
WRING = 3
QUARTERS = (2, 3, 0, 1)
EPS = 1e-12

L1ROWS = (slice(0, HR_), slice(HR_, P))
L0ROWS = (slice(HR_, P), slice(0, HR_))
E0ROWS = (slice(HR_, HR_ + LR), slice(0, LR))
E1ROWS = (slice(HR_ + LR, P), slice(LR, 2 * LR))


def two_layer_adapter_lora(nc, x_in, id0_row, all_ids, a0, b0_tab, ab1_tab, w0, w1, exp0, exp0_rows,
                           exp1_in, exp1_rows, bias, identity, marks, out):
    with ExitStack() as ctx:
        def sb(name, shape, dt=F32):
            return ctx.enter_context(nc.sbuf_tensor(name, shape, dt))

        def split(name, shape):
            return sb(name + "_hi", shape, F32R), sb(name + "_lo", shape, F32R)

        def sem(name):
            return ctx.enter_context(nc.semaphore(name))

        def bank(name):
            return ctx.enter_context(nc.psum_tensor(name, [P, 512], F32))

        xraw = [sb(f"xraw{i}", [P, KT, TOK]) for i in range(2)]
        slots = [t[:, KC * i:KC * (i + 1), :].rearrange("p k t -> p (k t)") for t in xraw for i in range(CH)]
        xs = split("xs", [P, KT, HALF])
        abraw = sb("abraw", [P, GROUP, 2, SLOT])
        b0raw = sb("b0raw", [P, GROUP, SLOT])
        bst = split("bst", [P, KT, 4, HR_])
        a1s = split("a1s", [P, KT, GROUP * RANK])
        w1s = split("w1s", [P, KT, D])
        m0s = split("m0s", [P, D])
        hr = sb("hr", [P, KT, 2, HC], F32R)
        m1x = split("m1x", [P, 2, D])
        k1 = split("k1", [P, TOK])
        k2 = split("k2", [P, TOK])
        c0s = split("c0s", [P, TOK])
        cm = sb("cm", [P, TOK])
        sel = sb("sel", [P, 2, P], F32R)
        hsb = sb("hsb", [P, 2, P])
        hb = hsb[:, 1, LR:LR + 1]
        hts = tuple(t[:, 0:P] for t in c0s)
        hls = split("hls", [P, 2, P])
        f0s = split("f0s", [P, FC])
        f1s = split("f1s", [P, 2, FC])
        exp1s = sb("exp1s", [P, KT, 2, FC], F32R)
        lp = sb("lp", [P, TT * P + HR_])
        lg = sb("lg", [P, TT, EXP])
        mx = sb("mx", [P, TT])
        ex = sb("ex", [P, TT, EXP])
        rs = sb("rs", [P, 2, TT])
        ident = sb("ident", [P, P])
        mark = sb("mark", [P, HALF + P], BF16)
        mask = mark[:, 0:HALF].rearrange("p (a t) -> p a t", a=1).to_broadcast([P, 2, HALF])
        adapter_of = mark[:, HALF:]
        idi = sb("idi", [P, 2, STEPS], I32)
        idf = sb("idf", [P, 2, STEPS])
        ids = sb("ids", [1, 2 * SEQS + EXP], I32)
        cb = sb("cb", [P, 2, EXP])
        bia = sb("bia", [P, 2, KT])
        bsum = sb("bsum", [P, KT])

        hr_hi, hr_lo = hr[:, :, 0, :], hr[:, :, 1, :]
        exp1_hi, exp1_lo = exp1s[:, :, 0, :], exp1s[:, :, 1, :]
        f1f = hsb[:, 0, 0:FC]

        a0raw = m0f = rows_raw = slots[SPARE]
        w0raw = [slots[k] if k < SPARE else slots[CH - 1] for k in range(KT)]
        w1raw = [slots[CH + k % WRING] for k in range(KT)]
        exp0_raw = lp[:, 0:EXP * PACK].rearrange("p (e n) -> p e n", e=EXP)
        exp0_zl = exp0_raw[:, :, 0:KT * (ER + 1)].rearrange("p e (k c) -> p e k c", k=KT)
        exp0_cols = exp0_raw[:, :, KT * (ER + 1):PACK - 2].rearrange("p e (k r) -> p e k r", k=KT)
        exp0_routerb, exp0_prior = exp0_raw[:, :, PACK - 2], exp0_raw[:, :, PACK - 1]
        exp0s = tuple(t[:, 0:KT * FC].rearrange("p (k c) -> p k c", c=FC) for t in c0s)
        exp1_raw = cm[:, 0:KT * FC].rearrange("p (k c) -> p k c", c=FC)
        w0s = tuple(m[:] for m in m1x)

        ps_p, ps_s, ps_z, ps_h, ps_t = (bank(n) for n in ("ps_p", "ps_s", "ps_z", "ps_h", "ps_t"))
        ps_d = [bank(f"ps_d{i}") for i in range(3)]
        z_of = [ps_z[:, i * TT * FC:(i + 1) * TT * FC].rearrange("p (j e c) -> p j e c", j=TT, e=EXP)
                for i in range(2)]
        ps_f = ps_h[:, 2 * HC:2 * HC + 2 * FC]

        ids_in, ident_in, marks_in, exp0_in, exp1_sem, rows_in, a0_in = (
            sem(n) for n in ("ids_in", "ident_in", "marks_in", "exp0_in", "exp1_in", "rows_in", "a0_in"))
        w0_in = [sem(f"w0_in{i}") for i in range(KT)]
        w1_in = [sem(f"w1_in{i}") for i in range(WRING)]
        x_in_sem = [sem(f"x_in{i}") for i in range(CH)]
        gathered = sem("gathered")
        stored = [sem(f"stored{i}") for i in range(CH)]
        init_done = sem("init_done")
        a0_hi, a0_lo, small_hi, small_lo, rows_hi, rows_lo = (
            sem(n) for n in ("a0_hi", "a0_lo", "small_hi", "small_lo", "rows_hi", "rows_lo"))
        w0_hi, w0_lo, w0_used, w1_hi, w1_lo = (
            sem(n) for n in ("w0_hi", "w0_lo", "w0_used", "w1_hi", "w1_lo"))
        m0_done, m0_hi, m0_copy, m0_lo, m0t_done, m0t_hi, m0t_lo = (
            sem(n) for n in ("m0_done", "m0_hi", "m0_copy", "m0_lo", "m0t_done", "m0t_hi", "m0t_lo"))
        f0_done, f0_hi, f0_lo, bias_step, ln_done = (
            sem(n) for n in ("f0_done", "f0_hi", "f0_lo", "bias_step", "ln_done"))
        x_hi, x_lo, x_lo_dve, x_used = (sem(n) for n in ("x_hi", "x_lo", "x_lo_dve", "x_used"))
        b_hi, b_lo, a_hi, a_lo = (sem(n) for n in ("b_hi", "b_lo", "a_hi", "a_lo"))
        cm_done, c0_hi, c0_lo, sel_built, sel_done = (
            sem(n) for n in ("cm_done", "c0_hi", "c0_lo", "sel_built", "sel_done"))
        k1_hi, k1_lo, h_done, h_sum, h_copied, ht_done, ht_hi, ht_lo = (
            sem(n) for n in ("k1_hi", "k1_lo", "h_done", "h_sum", "h_copied", "ht_done", "ht_hi", "ht_lo"))
        m1_done, m1_hi, m1_lo, f1_done, f1_sum, f1_hi, f1_lo = (
            sem(n) for n in ("m1_done", "m1_hi", "m1_lo", "f1_done", "f1_sum", "f1_hi", "f1_lo"))
        z_done, sm_step, exp_done, alpha_done, l_done, t_done, l_hi, l_lo = (
            sem(n) for n in ("z_done", "sm_step", "exp_done", "alpha_done", "l_done", "t_done", "l_hi", "l_lo"))
        q_done, qm_done, c1_done, c1_hi, c1_lo = (
            sem(n) for n in ("q_done", "qm_done", "c1_done", "c1_hi", "c1_lo"))
        d_done, d_out = sem("d_done"), sem("d_out")

        block = ctx.enter_context(nc.Block())

        def steps(eng, body, apart=1):
            body(0, 0, False)
            with eng.Fori(0, (STEPS - 1 - apart) // 2) as turn:
                for u in range(2):
                    body(2 * turn + (u + 1), (u + 1) % 2, False)
            for g in range(STEPS - apart, STEPS):
                body(g, g % 2, g == STEPS - 1)

        def b_quarter(tensor, q):
            return tensor[:, :, q, :].rearrange("p k (b r) -> p b k r", b=HSEQ)

        def b_raw(q):
            seqs = slice(0, HSEQ) if q >= 2 else slice(HSEQ, GROUP)
            raw = abraw[:, seqs, 0, :] if q in (1, 2) else b0raw[:, seqs, :]
            return raw.rearrange("p b (k r) -> p b k r", k=KT)

        a_raw = abraw[:, :, 1, :].rearrange("p b (k r) -> p b k r", k=KT)

        def after_step(eng, signal, count):
            if not (isinstance(count, int) and count == 0):
                eng.wait_ge(signal, count)

        @block.sync
        def _(sp):
            def load_x(g, par, i):
                sp.dma_start(xraw[par][:, KC * i:KC * (i + 1), :],
                             x_in[bass.ds(g, 1), :, KC * i:KC * (i + 1), :]
                             .rearrange("a p k t -> p (a k) t")).then_inc(x_in_sem[i], 16)

            def pick(g):
                return [(sp.value_load(ids[0:1, bass.ds(g * GROUP + b, 1)], min_val=0, max_val=ADAPT0 - 1),
                         sp.value_load(ids[0:1, bass.ds(g * GROUP + (SEQS + b), 1)],
                                       min_val=0, max_val=SEQS - 1)) for b in range(GROUP)]

            def gather(picks, seqs):
                for b in seqs:
                    n0, n1 = picks[b]
                    sp.dma_start(b0raw[:, b, :],
                                 b0_tab[bass.ds(n0, 1)].rearrange("a p n -> p (a n)")).then_inc(gathered, 16)
                    sp.dma_start(abraw[:, b, :, :].rearrange("p a n -> p (a n)"),
                                 ab1_tab[bass.ds(n1, 1)].rearrange("a p n -> p (a n)")).then_inc(gathered, 16)

            def expert(e):
                return sp.value_load(ids[0:1, 2 * SEQS + e:2 * SEQS + e + 1], min_val=0, max_val=15)

            sp.dma_start(ids[:], all_ids).then_inc(ids_in, 16)
            sp.dma_start(a0raw, a0).then_inc(a0_in, 16)
            for k in range(KT):
                if k == SPARE:
                    sp.wait_ge(w0_lo, CH)
                sp.dma_start(w0raw[k], w0[k]).then_inc(w0_in[k], 16)
                if k == 2:
                    sp.wait_ge(ids_in, 16)
                    experts = [expert(e) for e in range(EXP)]
                    for e, n in enumerate(experts):
                        sp.dma_start(exp0_raw[:, e, :], exp0[bass.ds(n, 1)].rearrange("a p n -> p (a n)")
                                     ).then_inc(exp0_in, 16)
                if k == 3:
                    sp.dma_start(ident[:], identity).then_inc(ident_in, 16)
                    sp.dma_start(exp1_raw.rearrange("p k c -> p (k c)"), exp1_in).then_inc(exp1_sem, 16)
                    sp.dma_start(bia[:], bias).then_inc(exp1_sem, 16)
                    picks = pick(0)
                if k >= 4:
                    gather(picks, range(2 * k - 8, 2 * k - 6))
            for i in range(CH):
                if i == CH - 1:
                    sp.wait_ge(w0_lo, KT)
                load_x(0, 0, i)
                if i == 0:
                    sp.dma_start(mark[:], marks).then_inc(marks_in, 16)
                    sp.dma_start(idi[:], id0_row).then_inc(marks_in, 16)
            for k in range(KT):
                if k >= WRING:
                    sp.wait_ge(w1_lo, k - WRING + 1)
                sp.dma_start(w1raw[k], w1[k]).then_inc(w1_in[k % WRING], 16)
            sp.wait_ge(m0t_done, 1)
            for e, n in enumerate(experts):
                r0 = E0ROWS[0].start + e * ER
                sp.dma_start(rows_raw[r0:r0 + ER, :],
                             exp0_rows[bass.ds(n, 1)].rearrange("a r o -> (a r) o")).then_inc(rows_in, 16)
            sp.dma_start(rows_raw[E1ROWS[0], :], exp1_rows).then_inc(rows_in, 16)
            picks = pick(1)
            sp.wait_ge(b_lo, 4)
            sp.wait_ge(a_lo, 1)
            gather(picks, range(GROUP))
            for i in range(CH):
                if i == 0:
                    sp.wait_ge(w1_lo, KT)
                if i == CH - 1:
                    sp.wait_ge(rows_lo, 2)
                load_x(1, 1, i)

            def body(g, par, last):
                ahead = not (isinstance(g, int) and g >= STEPS - 2)
                if ahead:
                    picks = pick(g + 2)
                for i in range(CH):
                    sp.wait_ge(d_out, KT * g + KC * (i + 1))
                    sp.dma_start(out[bass.ds(g, 1), :, KC * i:KC * (i + 1), :]
                                 .rearrange("a p k t -> p (a k) t"),
                                 xraw[par][:, KC * i:KC * (i + 1), :]).then_inc(stored[i], 16)
                    if ahead:
                        if i == 0:
                            sp.wait_ge(a_lo, g + 2)
                        else:
                            sp.wait_ge(stored[i - 1], 16 * g + 16)
                            load_x(g + 2, par, i - 1)
                        gather(picks, range(2 * i, 2 * i + 2))
                if ahead:
                    sp.wait_ge(stored[CH - 1], 16 * g + 16)
                    load_x(g + 2, par, CH - 1)

            steps(sp, body, 3)
            for i in range(CH):
                sp.wait_ge(stored[i], 16 * STEPS)

        @block.tensor
        def _(pe):
            def product(acc, left, right, first=True, final=True):
                (lh, ll), (rh, rl) = left, right
                pe.matmul(acc, lh, rh, start=first, stop=False, skip_group_check=True)
                pe.matmul(acc, lh, rl, start=False, stop=False, skip_group_check=True)
                return pe.matmul(acc, ll, rh, start=False, stop=final, skip_group_check=True)

            def stacked(acc, high, low, right, k):
                n = right.shape[-1]
                pe.matmul(acc, high, right.rearrange("p a n -> p (a n)"), start=(k == 0), stop=False,
                          skip_group_check=True)
                return pe.matmul(acc[:, 0:n], low, right[:, 0, :], start=False, stop=(k == KT - 1),
                                 skip_group_check=True)

            def part(pair, *index):
                return tuple(t[index] for t in pair)

            ALL = slice(None)

            def project(g, half):
                if half == 0:
                    pe.wait_ge(b_lo, 4 * g + 4)
                    after_step(pe, cm_done, g)
                for kc in range(CH):
                    first_step = isinstance(g, int) and g == 0
                    if half == 0 or first_step:
                        pe.wait_ge(x_lo, (CH * half if first_step else 6 * g + 2) + kc + 1)
                    elif kc % 2 == 0:
                        pe.wait_ge(x_lo, 6 * g + 6 + kc // 2 + 1)
                    else:
                        pe.wait_ge(x_lo_dve, 2 * g + (kc // 2 - 1))
                    for k in range(KC * kc, KC * (kc + 1)):
                        cols = tuple(t[:, k, 2 - 2 * half:4 - 2 * half, :].rearrange("p a n -> p (a n)")
                                     for t in bst)
                        mm = product(ps_p[:, half * HALF:(half + 1) * HALF], cols, part(xs, ALL, k, ALL),
                                     k == 0, k == KT - 1)
                    mm.then_inc(x_used, 1)

            pe.wait_ge(a0_lo, 1)
            for k in range(KT):
                pe.wait_ge(w0_lo, k + 1)
                for h in range(2):
                    mm = product(ps_d[h][:], part(a1s, ALL, k, ALL),
                                 tuple(w[:, k % 2, h * 512:(h + 1) * 512] for w in w0s), k == 0, k == KT - 1)
                mm.then_inc(w0_used, 1)
            pe.wait_ge(small_lo, 1)
            for k in range(KT):
                mm = product(ps_z[:, 0:FC], part(a1s, ALL, k, ALL), part(exp0s, ALL, k, ALL),
                             k == 0, k == KT - 1)
            mm.then_inc(f0_done, 1)
            pe.wait_ge(m0_copy, 2)
            pe.wait_ge(ident_in, 16)
            for k in range(KT):
                to = ps_d[2] if k < KT // 2 else ps_t
                mm = pe.transpose(to[:, (k % 4) * P:(k % 4 + 1) * P], m0f[:, k * P:(k + 1) * P], ident[:])
            mm.then_inc(m0t_done, 1)
            project(0, 0)
            project(0, 1)
            pe.wait_ge(m0t_lo, 2)
            pe.wait_ge(small_lo, 4)
            pe.wait_ge(init_done, 2)

            def body(g, par, last):
                after_step(pe, f1_lo, 2 * g)
                for k in range(KT):
                    high, low = (t[:, k, 1:3, :].rearrange("p a n -> p (a n)") for t in bst)
                    mm = stacked(ps_h[:, 0:2 * HC], high, low, hr[:, k, :, :], k)
                mm.then_inc(h_done, 1)
                pe.wait_ge(sel_built, 2 * g + 2)
                pe.wait_ge(c0_lo, g + 1)
                after_step(pe, c1_done, g)
                for half in range(2):
                    cols = slice(half * HALF, (half + 1) * HALF)
                    pe.matmul(ps_s[:, cols], sel[:, half, :], c0s[0][:, cols], start=True, stop=False,
                              skip_group_check=True)
                    mm = pe.matmul(ps_s[:, cols], sel[:, half, :], c0s[1][:, cols], start=False, stop=True,
                                   skip_group_check=True)
                mm.then_inc(sel_done, 1)

                def wide(h):
                    for k in range(KT):
                        if isinstance(g, int) and g == 0 and h == 0:
                            pe.wait_ge(w1_lo, k + 1)
                        mm = product(ps_d[h][:], part(a1s, ALL, k, ALL),
                                     part(w1s, ALL, k, slice(h * 512, (h + 1) * 512)), k == 0, k == KT - 1)
                    mm.then_inc(m1_done, 1)

                def route(layer, coefs, weights):
                    for j in range(TT):
                        w = part(weights, ALL, j // 2, ALL) if layer else part(weights, ALL, ALL)
                        at = layer * TT * FC + j * FC
                        mm = product(ps_z[:, at:at + FC], part(coefs, ALL, slice(j * P, (j + 1) * P)), w)
                    mm.then_inc(z_done, 1)

                def turn():
                    for j in range(TT):
                        at = j * P + (j // 2) * HR_
                        mm = pe.transpose(ps_t[:, j * P:(j + 1) * P], lp[:, at:at + P], ident[:])
                    mm.then_inc(t_done, 1)

                pe.wait_ge(a_lo, g + 1)
                after_step(pe, d_out, KT * g)
                wide(0)
                pe.wait_ge(h_copied, g + 1)
                after_step(pe, l_lo, 4 * g)
                pe.transpose(ps_t[:, 0:P], hsb[:, 0, :], ident[:])
                pe.transpose(ps_t[:, P:2 * P], hsb[:, 1, :], ident[:]).then_inc(ht_done, 1)
                pe.wait_ge(k1_lo, g + 1)
                pe.wait_ge(f0_lo, 1)
                after_step(pe, l_done, 2 * g)
                route(0, k1, f0s)
                wide(1)
                pe.wait_ge(l_done, 2 * g + 1)
                pe.wait_ge(ht_lo, g + 1)
                turn()
                product(ps_s[:], part(hts, ALL, ALL), part(k1, ALL, ALL), True, False)
                for k in range(KT):
                    mm = stacked(ps_f, a1s[0][:, k, :], a1s[1][:, k, :], exp1s[:, k, :, :], k)
                mm.then_inc(f1_done, 1)
                pe.wait_ge(l_lo, 4 * g + 2)
                for half in range(2):
                    cols = slice(half * HALF, (half + 1) * HALF)
                    mm = product(ps_s[:, cols], part(hls, ALL, half, ALL), part(k2, ALL, cols), False, True)
                mm.then_inc(q_done, 1)
                if not last:
                    project(g + 1, 0)
                pe.wait_ge(c1_lo, 2 * g + 2)
                pe.wait_ge(f1_lo, 2 * g + 2)
                route(1, k2, f1s)
                if not last:
                    project(g + 1, 1)
                pe.wait_ge(l_done, 2 * g + 2)
                turn()

                def from_layer0(m):
                    product(ps_d[m % 3][:], part(m0s, ALL, slice(m * P, (m + 1) * P)), part(k1, ALL, ALL),
                            True, False)

                pe.wait_ge(m1_lo, 4 * g + 4)
                for m in range(3):
                    from_layer0(m)
                pe.wait_ge(l_lo, 4 * g + 4)
                for m in range(KT):
                    if m >= 3:
                        pe.wait_ge(d_out, KT * g + m - 2)
                        from_layer0(m)
                    for half in range(2):
                        cols = slice(half * HALF, (half + 1) * HALF)
                        mm = product(ps_d[m % 3][:, cols], part(m1x, ALL, half, slice(m * P, (m + 1) * P)),
                                     part(k2, ALL, cols), False, True)
                    mm.then_inc(d_done, 1)

            steps(pe, body)

        @block.scalar
        def _(act):
            def copy(dst, src):
                return act.activation(dst, src, ACT.Copy)

            def split_x(g, par, half, chunks=range(CH)):
                n = 2 * g + half
                for i in chunks:
                    act.wait_ge(x_in_sem[i], 16 * g + 16)
                    if not (isinstance(n, int) and n == 0):
                        act.wait_ge(x_used, CH * n + (i + 1 - CH))
                    copy(xs[0][:, KC * i:KC * (i + 1), :],
                         xraw[par][:, KC * i:KC * (i + 1), half * HALF:(half + 1) * HALF]).then_inc(x_hi, 1)

            def split_b(g):
                act.wait_ge(gathered, 16 * 2 * GROUP * (g + 1))
                for q in QUARTERS:
                    copy(b_quarter(bst[0], q), b_raw(q)).then_inc(b_hi, 1)

            def split_a(g):
                act.wait_ge(gathered, 16 * 2 * GROUP * (g + 1))
                copy(a1s[0][:].rearrange("p k (b r) -> p b k r", b=GROUP), a_raw).then_inc(a_hi, 1)

            def c0_high(g):
                act.wait_ge(cm_done, g + 1)
                copy(c0s[0][:], cm[:]).then_inc(c0_hi, 1)

            act.wait_ge(a0_in, 16)
            copy(a1s[0][:].rearrange("p k n -> p (k n)"), a0raw).then_inc(a0_hi, 1)
            for k in range(KT):
                act.wait_ge(w0_in[k], 16)
                if k >= 2:
                    act.wait_ge(w0_used, k - 1)
                copy(w0s[0][:, k % 2, :], w0raw[k]).then_inc(w0_hi, 1)
                if k == 4:
                    act.wait_ge(exp0_in, 16 * EXP)
                    copy(exp0s[0].rearrange("p k (e c) -> p e k c", e=EXP), exp0_zl).then_inc(small_hi, 1)
                    copy(hr_hi[:, :, P:P + LR].rearrange("p k (e r) -> p e k r", e=EXP), exp0_cols
                         ).then_inc(small_hi, 1)
                if k == 6:
                    act.wait_ge(exp1_sem, 32)
                    copy(exp1_hi, exp1_raw).then_inc(small_hi, 1)
                    copy(hr_hi[:, :, P + LR:P + LR + 1], bia[:, 0, :].rearrange("p (k a) -> p k a", a=1)
                         ).then_inc(small_hi, 1)
            act.wait_ge(w0_used, KT)
            act.wait_ge(a0_lo, 1)
            for h in range(2):
                copy(m0s[0][:, h * 512:(h + 1) * 512], ps_d[h][:]).then_inc(m0_hi, 1)
                copy(m0f[:, h * 512:(h + 1) * 512], ps_d[h][:]).then_inc(m0_copy, 1)
            act.wait_ge(f0_done, 1)
            copy(f0s[0][:], ps_z[:, 0:FC]).then_inc(f0_hi, 1)
            split_b(0)
            act.wait_ge(m0t_done, 1)
            for h, src in enumerate((ps_d[2], ps_t)):
                copy(hr_hi[:, 4 * h:4 * h + 4, 0:P], src[:].rearrange("p (k n) -> p k n", n=P)
                     ).then_inc(m0t_hi, 1)
            split_x(0, 0, 0)
            split_a(0)
            act.wait_ge(bias_step, 2)
            act.activation(cb[:, 1, :], cb[:, 0, :], ACT.Ln).then_inc(ln_done, 1)
            for k in range(KT):
                act.wait_ge(w1_in[k % WRING], 16 * (k // WRING + 1))
                copy(w1s[0][:, k, :], w1raw[k]).then_inc(w1_hi, 1)
                if k < CH:
                    split_x(0, 0, 1, [k])
                if k == 5:
                    c0_high(0)
            act.wait_ge(rows_in, 16 * (EXP + 1))
            for half in range(2):
                copy(m1x[0][L0ROWS[half], half, :], rows_raw[L0ROWS[0], :]).then_inc(rows_hi, 1)

            def body(g, par, last):
                act.wait_ge(h_sum, 2 * g + 2)
                copy(hsb[:, 1, HR_:HR_ + LR], hsb[:, 1, 0:LR]).then_inc(h_copied, 1)
                act.wait_ge(sel_done, g + 1)
                copy(k1[0][:], ps_s[:]).then_inc(k1_hi, 1)
                act.wait_ge(m1_done, 2 * g + 1)

                def wide_high(h):
                    for half in range(2):
                        copy(m1x[0][L1ROWS[half], half, h * 512:(h + 1) * 512],
                             ps_d[h][L1ROWS[half], :]).then_inc(m1_hi, 1)

                def coef_high(layer):
                    act.wait_ge(t_done, 2 * g + layer + 1)
                    for half in range(2):
                        rows, cols = (E0ROWS, E1ROWS)[layer][half], slice(half * HALF, (half + 1) * HALF)
                        copy(k2[0][rows, cols], ps_t[rows, cols]).then_inc(l_hi, 1)

                def softmax_exp(layer):
                    act.wait_ge(sm_step, 10 * g + 5 * layer + 3)
                    act.activation(ex[:], lg[:], ACT.Exp).then_inc(exp_done, 1)

                wide_high(0)
                act.wait_ge(ht_done, g + 1)
                copy(hts[0][:], ps_t[:, 0:P]).then_inc(ht_hi, 1)
                for half in range(2):
                    rows = E0ROWS[half]
                    copy(hls[0][rows, half, :], ps_t[rows, P:2 * P]).then_inc(ht_hi, 1)
                softmax_exp(0)
                if not last:
                    split_b(g + 1)
                    split_x(g + 1, 1 - par, 0)
                coef_high(0)
                act.wait_ge(m1_done, 2 * g + 2)
                wide_high(1)
                act.wait_ge(f1_sum, g + 1)
                for half in range(2):
                    copy(f1s[0][L1ROWS[half], half, :], f1f[L1ROWS[half], :]).then_inc(f1_hi, 1)
                act.wait_ge(c1_done, g + 1)
                for half in range(2):
                    cols = slice(half * HALF, (half + 1) * HALF)
                    copy(k2[0][L1ROWS[half], cols], cm[L1ROWS[half], cols]).then_inc(c1_hi, 1)
                if not last:
                    split_x(g + 1, 1 - par, 1)
                softmax_exp(1)
                if not last:
                    split_a(g + 1)
                coef_high(1)
                if not last:
                    c0_high(g + 1)

            steps(act, body)

        @block.vector
        def _(dve):
            def low(dst, whole, high):
                return dve.tensor_tensor(dst, whole, high.bitcast(F32), ALU.subtract)

            def masked(g):
                dve.wait_ge(x_used, 2 * CH * (g + 1))
                dve.tensor_tensor(cm[:].rearrange("p (a t) -> p a t", a=2),
                                  ps_p[:].rearrange("p (a t) -> p a t", a=2), mask, ALU.mult).then_inc(cm_done, 1)

            def select(g):
                after_step(dve, sel_done, g)
                for half in range(2):
                    dve.tensor_scalar(sel[:, half, :], adapter_of, idf[:, half, bass.ds(g, 1)], None,
                                      ALU.is_equal).then_inc(sel_built, 1)

            def c0_low(g):
                dve.wait_ge(c0_hi, g + 1)
                low(c0s[1][:], cm[:], c0s[0][:]).then_inc(c0_lo, 1)

            def split_b(g):
                for n, q in enumerate(QUARTERS):
                    dve.wait_ge(b_hi, 4 * g + n + 1)
                    low(b_quarter(bst[1], q), b_raw(q), b_quarter(bst[0], q)).then_inc(b_lo, 1)

            def split_x_odd(g, par):
                for i in (1, 3):
                    dve.wait_ge(x_hi, 2 * CH * g + CH + i + 1)
                    low(xs[1][:, KC * i:KC * (i + 1), :], xraw[par][:, KC * i:KC * (i + 1), HALF:],
                        xs[0][:, KC * i:KC * (i + 1), :]).then_inc(x_lo_dve, 1)

            for t in (*hls, *f1s, *k2):
                dve.memset(t[:].bitcast(F32), 0.0)
            dve.memset(hr[:, :, :, HC - 1:HC].bitcast(F32), 0.0)
            dve.memset(hsb[:, 1, :], 0.0).then_inc(init_done, 1)
            dve.wait_ge(a0_hi, 1)
            low(a1s[1][:].rearrange("p k n -> p (k n)"), a0raw, a1s[0][:].rearrange("p k n -> p (k n)")
                ).then_inc(a0_lo, 1)
            for k in range(KT):
                dve.wait_ge(w0_hi, k + 1)
                low(w0s[1][:, k % 2, :], w0raw[k], w0s[0][:, k % 2, :]).then_inc(w0_lo, 1)
                if k == 4:
                    dve.wait_ge(small_hi, 2)
                    low(exp0s[1].rearrange("p k (e c) -> p e k c", e=EXP), exp0_zl,
                        exp0s[0].rearrange("p k (e c) -> p e k c", e=EXP)).then_inc(small_lo, 1)
                    low(hr_lo[:, :, P:P + LR].rearrange("p k (e r) -> p e k r", e=EXP), exp0_cols,
                        hr_hi[:, :, P:P + LR].rearrange("p k (e r) -> p e k r", e=EXP)).then_inc(small_lo, 1)
                if k == 6:
                    dve.wait_ge(small_hi, 4)
                    low(exp1_lo, exp1_raw, exp1_hi).then_inc(small_lo, 1)
                    low(hr_lo[:, :, P + LR:P + LR + 1], bia[:, 0, :].rearrange("p (k a) -> p k a", a=1),
                        hr_hi[:, :, P + LR:P + LR + 1]).then_inc(small_lo, 1)
            for h in range(2):
                dve.wait_ge(m0_copy, h + 1)
                low(m0s[1][:, h * 512:(h + 1) * 512], ps_d[h][:], m0s[0][:, h * 512:(h + 1) * 512]
                    ).then_inc(m0_lo, 1)
            dve.tensor_tensor(bsum[:], bia[:, 0, :], bia[:, 1, :], ALU.add).then_inc(bias_step, 1)
            dve.tensor_scalar(cb[:, 0, :], exp0_prior, EPS, None, ALU.add).then_inc(bias_step, 1)
            dve.wait_ge(f0_hi, 1)
            low(f0s[1][:], ps_z[:, 0:FC], f0s[0][:]).then_inc(f0_lo, 1)
            split_b(0)
            for h, src in enumerate((ps_d[2], ps_t)):
                dve.wait_ge(m0t_hi, h + 1)
                low(hr_lo[:, 4 * h:4 * h + 4, 0:P], src[:].rearrange("p (k n) -> p k n", n=P),
                    hr_hi[:, 4 * h:4 * h + 4, 0:P]).then_inc(m0t_lo, 1)
            dve.wait_ge(ln_done, 1)
            dve.tensor_tensor(cb[:, 0, :], cb[:, 1, :], exp0_routerb, ALU.add).then_inc(bias_step, 1)
            dve.wait_ge(bias_step, 3)
            dve.memset(lp[:], 0.0).then_inc(init_done, 1)
            dve.wait_ge(marks_in, 32)
            dve.tensor_copy(idf[:], idi[:]).then_inc(bias_step, 1)
            for k in range(KT):
                dve.wait_ge(w1_hi, k + 1)
                low(w1s[1][:, k, :], w1raw[k], w1s[0][:, k, :]).then_inc(w1_lo, 1)
                if k == 5:
                    dve.wait_ge(bias_step, 4)
                    masked(0)
                    select(0)
                    c0_low(0)
            dve.wait_ge(rows_hi, 2)
            for half in range(2):
                low(m1x[1][L0ROWS[half], half, :], rows_raw[L0ROWS[0], :], m1x[0][L0ROWS[0], 0, :]
                    ).then_inc(rows_lo, 1)
            dve.wait_ge(init_done, 2)

            def body(g, par, last):
                whole = hsb[:].rearrange("p a n -> p (a n)")
                dve.wait_ge(h_done, g + 1)
                for half in range(2):
                    dve.tensor_reduce(whole[L1ROWS[half], 0:HC],
                                      ps_h[L1ROWS[1 - half], 0:2 * HC].rearrange("p (a n) -> p n a", a=2),
                                      AX.X, ALU.add).then_inc(h_sum, 1)
                dve.wait_ge(k1_hi, g + 1)
                low(k1[1][:], ps_s[:], k1[0][:]).then_inc(k1_lo, 1)

                def wide_low(h):
                    for half in range(2):
                        dve.wait_ge(m1_hi, 4 * g + 2 * h + half + 1)
                        low(m1x[1][L1ROWS[half], half, h * 512:(h + 1) * 512], ps_d[h][L1ROWS[half], :],
                            m1x[0][L1ROWS[half], half, h * 512:(h + 1) * 512]).then_inc(m1_lo, 1)

                def coef_low(layer):
                    for half in range(2):
                        rows, cols = (E0ROWS, E1ROWS)[layer][half], slice(half * HALF, (half + 1) * HALF)
                        dve.wait_ge(l_hi, 4 * g + 2 * layer + half + 1)
                        low(k2[1][rows, cols], ps_t[rows, cols], k2[0][rows, cols]).then_inc(l_lo, 1)

                def softmax(layer):
                    z = z_of[layer]
                    at = 10 * g + 5 * layer
                    dve.wait_ge(z_done, 2 * g + layer + 1)
                    if layer == 0:
                        dve.tensor_tensor(lg[:], z[:, :, :, ER],
                                          cb[:, 0:1, :].to_broadcast([P, TT, EXP]), ALU.add).then_inc(sm_step, 1)
                    else:
                        dve.tensor_copy(lg[:], z[:, :, :, ER]).then_inc(sm_step, 1)
                    dve.wait_ge(sm_step, at + 1)
                    dve.tensor_reduce(mx[:], lg[:], AX.X, ALU.max).then_inc(sm_step, 1)
                    dve.wait_ge(sm_step, at + 2)
                    dve.tensor_tensor(lg[:], lg[:],
                                      mx[:].rearrange("p (j a) -> p j a", a=1).to_broadcast([P, TT, EXP]),
                                      ALU.subtract).then_inc(sm_step, 1)
                    dve.wait_ge(exp_done, 2 * g + layer + 1)
                    dve.tensor_reduce(rs[:, 0, :], ex[:], AX.X, ALU.add).then_inc(sm_step, 1)
                    dve.wait_ge(sm_step, at + 4)
                    dve.reciprocal(rs[:, 1, :], rs[:, 0, :]).then_inc(sm_step, 1)
                    dve.wait_ge(sm_step, at + 5)
                    dve.scalar_tensor_tensor(out=lg[:], in0=ex[:], scalar=2.0,
                                             in1=rs[:, 1, :].rearrange("p (j a) -> p j a", a=1)
                                             .to_broadcast([P, TT, EXP]),
                                             op0=ALU.mult, op1=ALU.mult).then_inc(alpha_done, 1)
                    dve.wait_ge(alpha_done, 2 * g + layer + 1)
                    to = lp[:, HR_:HR_ + TT * P].rearrange("p (j e r) -> p j e r", j=TT, r=ER)[
                        :, :, layer * EXP:(layer + 1) * EXP, :]
                    dve.tensor_tensor(to, z[:, :, :, 0:ER],
                                      lg[:].rearrange("p j (e a) -> p j e a", a=1)
                                      .to_broadcast([P, TT, EXP, ER]), ALU.mult).then_inc(l_done, 1)

                wide_low(0)
                dve.wait_ge(ht_hi, 3 * g + 3)
                low(hts[1][:], ps_t[:, 0:P], hts[0][:])
                for half in range(2):
                    rows = E0ROWS[half]
                    ins = low(hls[1][rows, half, :], ps_t[rows, P:2 * P], hls[0][rows, half, :])
                ins.then_inc(ht_lo, 1)
                softmax(0)
                if not last:
                    split_b(g + 1)
                coef_low(0)
                dve.wait_ge(f1_done, g + 1)
                dve.tensor_reduce(f1f, ps_f.rearrange("p (a n) -> p n a", a=2), AX.X, ALU.add
                                  ).then_inc(f1_sum, 1)
                for half in range(2):
                    dve.wait_ge(f1_hi, 2 * g + half + 1)
                    low(f1s[1][L1ROWS[half], half, :], f1f[L1ROWS[half], :], f1s[0][L1ROWS[half], half, :]
                        ).then_inc(f1_lo, 1)
                dve.wait_ge(q_done, g + 1)
                q = ps_s[:].rearrange("p (a t) -> p a t", a=2)
                dve.scalar_tensor_tensor(out=q, in0=q, scalar=hb, in1=mask,
                                         op0=ALU.add, op1=ALU.mult).then_inc(qm_done, 1)
                dve.wait_ge(qm_done, g + 1)
                dve.tensor_tensor(cm[:], cm[:], ps_s[:], ALU.add).then_inc(c1_done, 1)
                for half in range(2):
                    cols = slice(half * HALF, (half + 1) * HALF)
                    dve.wait_ge(c1_hi, 2 * g + half + 1)
                    low(k2[1][L1ROWS[half], cols], cm[L1ROWS[half], cols], k2[0][L1ROWS[half], cols]
                        ).then_inc(c1_lo, 1)
                wide_low(1)
                if not last:
                    split_x_odd(g + 1, 1 - par)
                softmax(1)
                coef_low(1)
                if not last:
                    masked(g + 1)
                for m in range(KT):
                    dve.wait_ge(d_done, KT * g + m + 1)
                    dve.scalar_tensor_tensor(out=xraw[par][:, m, :], in0=ps_d[m % 3][:],
                                             scalar=bsum[:, m:m + 1], in1=xraw[par][:, m, :],
                                             op0=ALU.add, op1=ALU.add).then_inc(d_out, 1)
                    if not last and m == 1:
                        select(g + 1)
                    if not last and m == 2:
                        c0_low(g + 1)

            steps(dve, body)

        @block.gpsimd
        def _(pool):
            def low(dst, whole, high):
                return pool.tensor_tensor(dst, whole, high.bitcast(F32), ALU.subtract)

            def split_x(g, par, half, chunks):
                for i in chunks:
                    pool.wait_ge(x_hi, 2 * CH * g + CH * half + i + 1)
                    low(xs[1][:, KC * i:KC * (i + 1), :],
                        xraw[par][:, KC * i:KC * (i + 1), half * HALF:(half + 1) * HALF],
                        xs[0][:, KC * i:KC * (i + 1), :]).then_inc(x_lo, 1)

            def split_a(g):
                pool.wait_ge(a_hi, g + 1)
                low(a1s[1][:].rearrange("p k (b r) -> p b k r", b=GROUP), a_raw,
                    a1s[0][:].rearrange("p k (b r) -> p b k r", b=GROUP)).then_inc(a_lo, 1)

            split_x(0, 0, 0, range(CH))
            split_a(0)
            split_x(0, 0, 1, range(CH))

            def body(g, par, last):
                if not last:
                    split_x(g + 1, 1 - par, 0, range(CH))
                    split_x(g + 1, 1 - par, 1, (0, 2))
                    split_a(g + 1)

            steps(pool, body)


def kernel(x, itok_B_3_7, itok_B_4_50, L0_cond_A, L0_cond_B, L0_ffn_W_base, L0_ffn_b_base, L0_ffn_lora_A,
           L0_ffn_lora_B, L0_ffn_router_W, L0_ffn_router_b, L0_ffn_domain_prior, L0_ffn_active, L1_cond_A,
           L1_cond_B, L1_ffn_W, L1_ffn_b, L1_ffn_A, L1_ffn_Bm, L1_ffn_Wr):
    import numpy as np
    import concourse.bacc as bacc
    from concourse.bass_utils import run_bass_kernel_spmd

    x, id0, id1, A0, B0, W0, b0, EA, EB, RW, Rb, prior, active, A1, B1, W1, b1, LA, LB, WR = (
        np.asarray(a) for a in (
            x, itok_B_3_7, itok_B_4_50, L0_cond_A, L0_cond_B, L0_ffn_W_base, L0_ffn_b_base, L0_ffn_lora_A,
            L0_ffn_lora_B, L0_ffn_router_W, L0_ffn_router_b, L0_ffn_domain_prior, L0_ffn_active, L1_cond_A,
            L1_cond_B, L1_ffn_W, L1_ffn_b, L1_ffn_A, L1_ffn_Bm, L1_ffn_Wr))

    def tiles(a):
        return np.swapaxes(a.reshape(*a.shape[:-1], KT, P), -1, -2)

    n_exp = EA.shape[0]
    rows = np.arange(P)
    seq_of_row, seq_of_col = rows % HR_ // RANK, np.arange(HALF) // LEN
    marks = np.concatenate([
        seq_of_row[:, None] == seq_of_col[None, :],
        np.where(rows[:, None] % RANK == rows[None, :] % RANK, rows[None, :] // RANK, -2),
    ], axis=1).astype(mybir.dt.np(BF16))
    row_ids = np.repeat(id0.reshape(STEPS, 2, HSEQ).transpose(1, 2, 0), RANK, axis=1)
    none = np.full_like(row_ids[0], -1)
    named = {
        "x_in": x.reshape(STEPS, TOK, KT, P).transpose(0, 3, 2, 1),
        "id0_row": np.stack([np.concatenate([none, row_ids[0]]), np.concatenate([row_ids[1], none])], axis=1),
        "all_ids": np.concatenate([id0, id1, active]).reshape(1, -1),
        "a0": tiles(A0.transpose(0, 2, 1)).transpose(2, 3, 0, 1).reshape(P, -1),
        "b0_tab": tiles(B0).transpose(0, 2, 3, 1).reshape(ADAPT0, P, -1),
        "ab1_tab": np.concatenate([tiles(B1).transpose(0, 2, 3, 1).reshape(SEQS, P, -1),
                                   A1.reshape(SEQS, KT, P, RANK).transpose(0, 2, 1, 3).reshape(SEQS, P, -1)],
                                  axis=2),
        "w0": W0.T.reshape(KT, P, D),
        "w1": W1.T.reshape(KT, P, D),
        "exp0": np.concatenate([
            tiles(np.concatenate([EA, RW[:, None, :]], axis=1)).transpose(0, 2, 3, 1).reshape(n_exp, P, -1),
            EB.reshape(n_exp, KT, P, ER).transpose(0, 2, 1, 3).reshape(n_exp, P, -1),
            np.repeat(np.stack([Rb, prior], axis=1)[:, None, :], P, axis=1)], axis=2),
        "exp0_rows": EB.transpose(0, 2, 1),
        "exp1_in": tiles(np.concatenate([LA, WR[:, None, :]], axis=1)).transpose(2, 3, 0, 1).reshape(P, -1),
        "exp1_rows": LB.transpose(0, 2, 1).reshape(LR, D),
        "bias": tiles(np.stack([b0, b1])).transpose(1, 0, 2),
        "identity": np.eye(P, dtype=np.float32),
        "marks": marks,
    }
    nc = bacc.Bacc("TRN2", target_bir_lowering=False, num_devices=1)
    arrays, args = {}, []
    for name, a in named.items():
        a = np.ascontiguousarray(a)
        arrays[name] = a
        args.append(nc.dram_tensor(name, a.shape, mybir.dt.from_np(a.dtype), kind="ExternalInput").ap())
    out = nc.dram_tensor("out", (STEPS, P, KT, TOK), F32, kind="ExternalOutput").ap()
    two_layer_adapter_lora(nc, *args, out)
    r = run_bass_kernel_spmd(nc, [arrays], core_ids=[0])
    y = r.results[0]["out"].reshape(STEPS, P, KT, TOK)
    return y.transpose(0, 3, 2, 1).reshape(SEQS, LEN, D)
```

```python
from contextlib import ExitStack

import concourse.bass as bass
from concourse import mybir

F32 = mybir.dt.float32
F32R = mybir.dt.float32r
BF16 = mybir.dt.bfloat16
I32 = mybir.dt.int32
ALU = mybir.AluOpType
ACT = mybir.ActivationFunctionType
AX = mybir.AxisListType

P = 128
D = 1024
KT = D // P
SEQS = 64
LEN = 64
RANK = 16
GROUP = 8
STEPS = SEQS // GROUP
TOK = GROUP * LEN
HALF = TOK // 2
HSEQ = GROUP // 2
HROWS = HSEQ * RANK
ADAPT0 = 8
EXP = 4
ER = 8
LR = EXP * ER
FC = EXP * (ER + 1)
HC = P + LR + 2
CH = 4
KC = KT // CH
TT = TOK // P
SLOT = KT * RANK
PACK = KT * (2 * ER + 1) + 2
SLOTS = 2 * CH
SPARE = SLOTS - 1
W1_SLOTS = (4, 5, 6, 7, 4, 5, 6, 4)
POOL_CHUNK = 5
WIDE = D + FC
WIDE_PARTS = ((slice(0, 384), 0), (slice(768, WIDE), 1), (slice(384, 768), 2))
F_PART = 1
F_AT = D - 768
QUARTERS = (2, 3, 0, 1)
EPS = 1e-12

L1ROWS = (slice(0, HROWS), slice(HROWS, P))
L0ROWS = (slice(HROWS, P), slice(0, HROWS))
E0ROWS = (slice(HROWS, HROWS + LR), slice(0, LR))
E1ROWS = (slice(HROWS + LR, P), slice(LR, 2 * LR))


def two_layer_adapter_lora(nc, x_in, id0_row, all_ids, a0, b0_tab, ab1_tab, w0, w1, exp0, exp0_rows,
                           exp1_in, exp1_rows, bias, identity, marks, out):
    with ExitStack() as ctx:
        def sb(name, shape, dt=F32):
            return ctx.enter_context(nc.sbuf_tensor(name, shape, dt))

        def split(name, shape):
            return sb(name + "_hi", shape, F32R), sb(name + "_lo", shape, F32R)

        def sem(name):
            return ctx.enter_context(nc.semaphore(name))

        def bank(name):
            return ctx.enter_context(nc.psum_tensor(name, [P, 512], F32))

        xraw = [sb(f"xraw{i}", [P, KT, TOK]) for i in range(2)]
        slots = [t[:, KC * i:KC * (i + 1), :].rearrange("p k t -> p (k t)") for t in xraw for i in range(CH)]
        xs = split("xs", [P, KT, HALF])
        abraw = sb("abraw", [P, GROUP, 2, SLOT])
        b0raw = sb("b0raw", [P, GROUP, SLOT])
        bst = split("bst", [P, KT, 4, HROWS])
        a1s = split("a1s", [P, KT, GROUP * RANK])
        w1s = split("w1s", [P, KT, WIDE])
        m0s = split("m0s", [P, D])
        hr = sb("hr", [P, KT, 2, HC], F32R)
        m1x = split("m1x", [P, 2, D])
        k1 = split("k1", [P, TOK])
        k2 = split("k2", [P, TOK])
        c0s = split("c0s", [P, TOK])
        cm = sb("cm", [P, TOK])
        sel = sb("sel", [P, 2, P], F32R)
        hsb = sb("hsb", [P, 2, P])
        hb = hsb[:, 1, LR:LR + 1]
        hts = tuple(t[:, 0:P] for t in c0s)
        hls = split("hls", [P, 2, P])
        f0s = sb("f0s", [P, 2, FC], F32R)
        f1s = sb("f1s", [P, 2, 2, FC], F32R)
        lp = sb("lp", [P, TT * P + HROWS])
        lg = sb("lg", [P, TT, EXP])
        mx = sb("mx", [P, TT])
        ex = sb("ex", [P, TT, EXP])
        rs = sb("rs", [P, 2, TT])
        ident = sb("ident", [P, P])
        mark = sb("mark", [P, HALF + P], BF16)
        mask = mark[:, 0:HALF].rearrange("p (a t) -> p a t", a=1).to_broadcast([P, 2, HALF])
        adapter_of = mark[:, HALF:]
        idi = sb("idi", [P, 2, STEPS], I32)
        idf = sb("idf", [P, 2, STEPS])
        ids = sb("ids", [1, 2 * SEQS + EXP], I32)
        cb = sb("cb", [P, 2, EXP])
        bia = sb("bia", [P, 2, KT])
        bsum = sb("bsum", [P, KT])

        hr_hi, hr_lo = hr[:, :, 0, :], hr[:, :, 1, :]
        exp1_hi, exp1_lo = (w[:, :, D:WIDE] for w in w1s)
        zs = hsb[:].rearrange("p a n -> p (a n)")[:, 0:TT * FC].rearrange("p (j e c) -> p j e c", j=TT, e=EXP)

        a0raw = b0raw[:].rearrange("p b n -> p (b n)")
        w0raw = slots
        m0f = rows_raw = slots[SPARE]
        w1raw = [slots[i] for i in W1_SLOTS]
        exp0_raw = lp[:, 0:EXP * PACK].rearrange("p (e n) -> p e n", e=EXP)
        exp0_zl = exp0_raw[:, :, 0:KT * (ER + 1)].rearrange("p e (k c) -> p e k c", k=KT)
        exp0_cols = exp0_raw[:, :, KT * (ER + 1):PACK - 2].rearrange("p e (k r) -> p e k r", k=KT)
        exp0_routerb, exp0_prior = exp0_raw[:, :, PACK - 2], exp0_raw[:, :, PACK - 1]
        exp0s = (exp1_hi, exp1_lo)
        exp1_raw = cm[:, 0:KT * FC].rearrange("p (k c) -> p k c", c=FC)
        a0s = a1s
        w0s = w1s

        ps_p, ps_s, ps_z, ps_h, ps_t = (bank(n) for n in ("ps_p", "ps_s", "ps_z", "ps_h", "ps_t"))
        ps_d = [bank(f"ps_d{i}") for i in range(3)]

        ids_in, ident_in, marks_in, exp0_in, exp1_sem, rows_in, a0_in = (
            sem(n) for n in ("ids_in", "ident_in", "marks_in", "exp0_in", "exp1_in", "rows_in", "a0_in"))
        w0_in = [sem(f"w0_in{i}") for i in range(KT)]
        w1_in = [sem(f"w1_in{i}") for i in range(KT)]
        x_in_sem = [sem(f"x_in{i}") for i in range(CH)]
        gathered = sem("gathered")
        stored = [sem(f"stored{i}") for i in range(CH)]
        init_done = sem("init_done")
        a0_hi, a0_lo, small_hi, small_lo, rows_hi, rows_lo = (
            sem(n) for n in ("a0_hi", "a0_lo", "small_hi", "small_lo", "rows_hi", "rows_lo"))
        w0_hi, w0_lo, w1_hi, w1_lo, w1_lo_pool = (
            sem(n) for n in ("w0_hi", "w0_lo", "w1_hi", "w1_lo", "w1_lo_pool"))
        m0_done, m0_hi, m0_copy, m0_lo, m0t_done, m0t_hi, m0t_lo = (
            sem(n) for n in ("m0_done", "m0_hi", "m0_copy", "m0_lo", "m0t_done", "m0t_hi", "m0t_lo"))
        bias_step, ln_done = sem("bias_step"), sem("ln_done")
        x_hi, x_lo, x_lo_dve, x_used = (sem(n) for n in ("x_hi", "x_lo", "x_lo_dve", "x_used"))
        b_hi, b_lo, a_hi, a_lo = (sem(n) for n in ("b_hi", "b_lo", "a_hi", "a_lo"))
        cm_done, c0_hi, c0_lo, sel_built, sel_done = (
            sem(n) for n in ("cm_done", "c0_hi", "c0_lo", "sel_built", "sel_done"))
        k1_hi, k1_lo, h_done, h_sum, h_copied, ht_done, ht_hi, ht_lo = (
            sem(n) for n in ("k1_hi", "k1_lo", "h_done", "h_sum", "h_copied", "ht_done", "ht_hi", "ht_lo"))
        m1_done, m1_hi, m1_lo, f1_lo = (sem(n) for n in ("m1_done", "m1_hi", "m1_lo", "f1_lo"))
        z_done, sm_step, exp_done, alpha_done, l_done, t_done, l_hi, l_lo = (
            sem(n) for n in ("z_done", "sm_step", "exp_done", "alpha_done", "l_done", "t_done", "l_hi", "l_lo"))
        z_sum, q_done, qm_done, c1_done, c1_hi, c1_lo = (
            sem(n) for n in ("z_sum", "q_done", "qm_done", "c1_done", "c1_hi", "c1_lo"))
        d_done, d_out = sem("d_done"), sem("d_out")

        block = ctx.enter_context(nc.Block())

        def steps(eng, body, apart=1):
            body(0, 0, False)
            with eng.Fori(0, (STEPS - 1 - apart) // 2) as turn:
                for u in range(2):
                    body(2 * turn + (u + 1), (u + 1) % 2, False)
            for g in range(STEPS - apart, STEPS):
                body(g, g % 2, g == STEPS - 1)

        def b_quarter(tensor, q):
            return tensor[:, :, q, :].rearrange("p k (b r) -> p b k r", b=HSEQ)

        def b_raw(q):
            seqs = slice(0, HSEQ) if q >= 2 else slice(HSEQ, GROUP)
            raw = abraw[:, seqs, 0, :] if q in (1, 2) else b0raw[:, seqs, :]
            return raw.rearrange("p b (k r) -> p b k r", k=KT)

        a_raw = abraw[:, :, 1, :].rearrange("p b (k r) -> p b k r", k=KT)

        def result_banks(last):
            return ps_d + [ps_p, ps_h] if last else ps_d

        def after_step(eng, signal, count):
            if not (isinstance(count, int) and count == 0):
                eng.wait_ge(signal, count)

        @block.sync
        def _(sp):
            def load_x(g, par, i):
                sp.dma_start(xraw[par][:, KC * i:KC * (i + 1), :],
                             x_in[bass.ds(g, 1), :, KC * i:KC * (i + 1), :]
                             .rearrange("a p k t -> p (a k) t")).then_inc(x_in_sem[i], 16)

            def values(first, count, limit):
                return nc.values_load_multi_w_load_instructions(
                    ids[0:1, bass.ds(first, count)], (mybir.EngineType.SP,), min_val=0, max_val=limit - 1)[1]

            def pick(g):
                return tuple(zip(values(g * GROUP, GROUP, ADAPT0), values(g * GROUP + SEQS, GROUP, SEQS)))

            def gather(picks, seqs):
                for b in seqs:
                    n0, n1 = picks[b]
                    sp.dma_start(b0raw[:, b, :],
                                 b0_tab[bass.ds(n0, 1)].rearrange("a p n -> p (a n)")).then_inc(gathered, 16)
                    sp.dma_start(abraw[:, b, :, :].rearrange("p a n -> p (a n)"),
                                 ab1_tab[bass.ds(n1, 1)].rearrange("a p n -> p (a n)")).then_inc(gathered, 16)

            sp.dma_start(ids[:], all_ids).then_inc(ids_in, 16)
            sp.dma_start(a0raw, a0).then_inc(a0_in, 16)
            for k in range(KT):
                sp.dma_start(w0raw[k], w0[k]).then_inc(w0_in[k], 16)
            sp.wait_ge(ids_in, 16)
            experts = values(2 * SEQS, EXP, 16)
            for e, n in enumerate(experts):
                sp.dma_start(exp0_raw[:, e, :], exp0[bass.ds(n, 1)].rearrange("a p n -> p (a n)")
                             ).then_inc(exp0_in, 16)
            picks = pick(0)
            sp.dma_start(ident[:], identity).then_inc(ident_in, 16)
            sp.wait_ge(a0_lo, 1)
            for i in range(CH):
                gather(picks, range(2 * i, 2 * i + 2))
                sp.wait_ge(w0_lo, i + 1)
                load_x(0, 0, i)
            sp.dma_start(mark[:], marks).then_inc(marks_in, 16)
            sp.dma_start(idi[:], id0_row).then_inc(marks_in, 16)
            for k in range(KT):
                if W1_SLOTS[k] in W1_SLOTS[:k]:
                    sp.wait_ge(w1_lo, max(j for j in range(k) if W1_SLOTS[j] == W1_SLOTS[k]) + 1)
                elif W1_SLOTS[k] == SPARE:
                    sp.wait_ge(m0t_done, 1)
                else:
                    sp.wait_ge(w0_lo, W1_SLOTS[k] + 1)
                sp.dma_start(w1raw[k], w1[k]).then_inc(w1_in[k], 16)
                if k == 2:
                    sp.dma_start(exp1_raw.rearrange("p k c -> p (k c)"), exp1_in).then_inc(exp1_sem, 16)
                    sp.dma_start(bia[:], bias).then_inc(exp1_sem, 16)
                    picks = pick(1)
                if k == 6:
                    sp.wait_ge(w1_lo, 4)
                    for e, n in enumerate(experts):
                        r0 = E0ROWS[0].start + e * ER
                        sp.dma_start(rows_raw[r0:r0 + ER, :],
                                     exp0_rows[bass.ds(n, 1)].rearrange("a r o -> (a r) o")
                                     ).then_inc(rows_in, 16)
                    sp.dma_start(rows_raw[E1ROWS[0], :], exp1_rows).then_inc(rows_in, 16)
            sp.wait_ge(b_lo, 4)
            sp.wait_ge(a_lo, 1)
            gather(picks, range(GROUP))
            sp.wait_ge(w1_lo, KT - 1)
            sp.wait_ge(w1_lo_pool, 1)
            for i in range(CH - 1):
                load_x(1, 1, i)
            sp.wait_ge(rows_lo, 2)
            load_x(1, 1, CH - 1)

            def body(g, par, last):
                ahead = not (isinstance(g, int) and g >= STEPS - 2)
                if ahead:
                    picks = pick(g + 2)
                    sp.wait_ge(a_lo, g + 2)
                    gather(picks, range(HSEQ))
                for i in range(CH):
                    if ahead and i in (1, 2):
                        gather(picks, range(HSEQ + 2 * i - 2, HSEQ + 2 * i))
                    sp.wait_ge(d_out, KT * g + KC * (i + 1))
                    sp.dma_start(out[bass.ds(g, 1), :, KC * i:KC * (i + 1), :]
                                 .rearrange("a p k t -> p (a k) t"),
                                 xraw[par][:, KC * i:KC * (i + 1), :]).then_inc(stored[i], 16)
                    if ahead and i > 0:
                        sp.wait_ge(stored[i - 1], 16 * g + 16)
                        load_x(g + 2, par, i - 1)
                if ahead:
                    sp.wait_ge(stored[CH - 1], 16 * g + 16)
                    load_x(g + 2, par, CH - 1)

            steps(sp, body, 3)
            for i in range(CH):
                sp.wait_ge(stored[i], 16 * STEPS)

        @block.tensor
        def _(pe):
            def product(acc, left, right, first=True, final=True):
                (lh, ll), (rh, rl) = left, right
                pe.matmul(acc, lh, rh, start=first, stop=False, skip_group_check=True)
                pe.matmul(acc, lh, rl, start=False, stop=False, skip_group_check=True)
                return pe.matmul(acc, ll, rh, start=False, stop=final, skip_group_check=True)

            def stacked(acc, high, low, right, first=True, final=True):
                n = right.shape[-1]
                pe.matmul(acc, high, right.rearrange("p a n -> p (a n)"), start=first, stop=False,
                          skip_group_check=True)
                return pe.matmul(acc[:, 0:n], low, right[:, 0, :], start=False, stop=final,
                                 skip_group_check=True)

            def part(pair, *index):
                return tuple(t[index] for t in pair)

            ALL = slice(None)

            def wide_product(n, adapters, weights, k):
                cols, at = WIDE_PARTS[n]
                return product(ps_d[at][:, 0:cols.stop - cols.start], part(adapters, ALL, k, ALL),
                               part(weights, ALL, k, cols), k == 0, k == KT - 1)

            def project(g, half):
                pe.wait_ge(b_lo, 4 * g + 2 * half + 2)
                if half == 0:
                    after_step(pe, cm_done, g)
                for kc in range(CH):
                    if half == 0:
                        pe.wait_ge(x_lo, 6 * g + kc + 1)
                    elif kc % 2 == 0:
                        pe.wait_ge(x_lo, 6 * g + CH + kc // 2 + 1)
                    else:
                        pe.wait_ge(x_lo_dve, 2 * g + kc // 2 + 1)
                    for k in range(KC * kc, KC * (kc + 1)):
                        cols = tuple(t[:, k, 2 - 2 * half:4 - 2 * half, :].rearrange("p a n -> p (a n)")
                                     for t in bst)
                        mm = product(ps_p[:, half * HALF:(half + 1) * HALF], cols, part(xs, ALL, k, ALL),
                                     k == 0, k == KT - 1)
                    mm.then_inc(x_used, 1)

            pe.wait_ge(a0_lo, 1)
            for k in range(KT):
                pe.wait_ge(w0_lo, k + 1)
                for n in (0, 2):
                    mm = wide_product(n, a0s, w0s, k)
            mm.then_inc(m0_done, 1)
            pe.wait_ge(m0_copy, 2)
            pe.wait_ge(ident_in, 16)

            def turn_m0(k):
                to = ps_s if k < KT // 2 else ps_t
                return pe.transpose(to[:, (k % 4) * P:(k % 4 + 1) * P], m0f[:, k * P:(k + 1) * P], ident[:])

            for k in range(6):
                turn_m0(k)
            pe.wait_ge(small_lo, 1)
            for k in range(KT):
                mm = wide_product(F_PART, a0s, w0s, k)
            mm.then_inc(m0_done, 1)
            pe.wait_ge(m0_copy, 3)
            for k in (6, 7):
                mm = turn_m0(k)
            mm.then_inc(m0t_done, 1)
            project(0, 0)
            project(0, 1)
            pe.wait_ge(m0t_lo, 2)
            pe.wait_ge(small_lo, 4)
            pe.wait_ge(init_done, 1)

            def body(g, par, last):
                after_step(pe, h_sum, 2 * g)
                for k in range(KT):
                    high, low = (t[:, k, 1:3, :].rearrange("p a n -> p (a n)") for t in bst)
                    mm = stacked(ps_h[:, 0:2 * HC], high, low, hr[:, k, :, :],
                                 k == 0, k == KT - 1)
                mm.then_inc(h_done, 1)
                pe.wait_ge(sel_built, 2 * g + 2)
                pe.wait_ge(c0_lo, g + 1)
                after_step(pe, c1_done, 2 * g)
                for half in range(2):
                    cols = slice(half * HALF, (half + 1) * HALF)
                    pe.matmul(ps_s[:, cols], sel[:, half, :], c0s[0][:, cols], start=True, stop=False,
                              skip_group_check=True)
                    mm = pe.matmul(ps_s[:, cols], sel[:, half, :], c0s[1][:, cols], start=False, stop=True,
                                   skip_group_check=True)
                mm.then_inc(sel_done, 1)

                def wide(n, chunks=range(KT)):
                    for k in chunks:
                        if isinstance(g, int) and g == 0 and n == 0:
                            if k == POOL_CHUNK:
                                pe.wait_ge(w1_lo_pool, 1)
                            else:
                                pe.wait_ge(w1_lo, k + 1 - (k > POOL_CHUNK))
                        mm = wide_product(n, a1s, w1s, k)
                    if k == KT - 1:
                        mm.then_inc(m1_done, 1)

                def route(layer, coefs, weights):
                    for j in range(TT):
                        if layer == 1 and j % 2 == 0:
                            pe.wait_ge(c1_lo, 2 * g + j // 2 + 1)
                        high, low = part(coefs, ALL, slice(j * P, (j + 1) * P))
                        mm = stacked(ps_z[:, j * 2 * FC:(j + 1) * 2 * FC], high, low,
                                     weights[:, j // 2, :, :] if layer else weights[:])
                    mm.then_inc(z_done, 1)

                def turn():
                    for j in range(TT):
                        at = j * P + (j // 2) * HROWS
                        mm = pe.transpose(ps_t[:, j * P:(j + 1) * P], lp[:, at:at + P], ident[:])
                    mm.then_inc(t_done, 1)

                pe.wait_ge(a_lo, g + 1)
                after_step(pe, d_out, KT * g)
                wide(0)
                pe.wait_ge(h_copied, g + 1)
                after_step(pe, l_lo, 4 * g)
                pe.transpose(ps_t[:, 0:P], hsb[:, 0, :], ident[:])
                pe.transpose(ps_t[:, P:2 * P], hsb[:, 1, :], ident[:]).then_inc(ht_done, 1)
                pe.wait_ge(k1_lo, g + 1)
                pe.wait_ge(m0_lo, len(WIDE_PARTS))
                after_step(pe, l_done, 2 * g)
                route(0, k1, f0s)
                wide(1)
                wide(2, range(KT // 2))
                pe.wait_ge(l_done, 2 * g + 1)
                pe.wait_ge(ht_lo, g + 1)
                turn()
                wide(2, range(KT // 2, KT))
                product(ps_s[:], part(hts, ALL, ALL), part(k1, ALL, ALL), True, False)
                pe.wait_ge(l_lo, 4 * g + 2)
                for half in range(2):
                    cols = slice(half * HALF, (half + 1) * HALF)
                    mm = product(ps_s[:, cols], part(hls, ALL, half, ALL), part(k2, ALL, cols), False, True)
                mm.then_inc(q_done, 1)
                banks = result_banks(last)

                def from_layer0(m):
                    product(banks[m % len(banks)][:], part(m0s, ALL, slice(m * P, (m + 1) * P)),
                            part(k1, ALL, ALL), True, False)

                def start_results(tiles):
                    for m in tiles:
                        if m < 3:
                            pe.wait_ge(m1_lo, 6 * g + (4, 4, 6)[m])
                        from_layer0(m)

                if last:
                    start_results((0, 1, 3))
                else:
                    project(g + 1, 0)
                pe.wait_ge(f1_lo, 2 * g + 2)
                route(1, k2, f1s)
                if last:
                    start_results((4, 2))
                else:
                    project(g + 1, 1)
                pe.wait_ge(l_done, 2 * g + 2)
                turn()
                if not last:
                    start_results(range(3))
                pe.wait_ge(l_lo, 4 * g + 4)
                for m in range(KT):
                    if m >= len(banks):
                        pe.wait_ge(d_out, KT * g + (m + 1 - len(banks)))
                        from_layer0(m)
                    for half in range(2):
                        cols = slice(half * HALF, (half + 1) * HALF)
                        mm = product(banks[m % len(banks)][:, cols],
                                     part(m1x, ALL, half, slice(m * P, (m + 1) * P)),
                                     part(k2, ALL, cols), False, True)
                    mm.then_inc(d_done, 1)

            steps(pe, body)

        @block.scalar
        def _(act):
            def copy(dst, src):
                return act.activation(dst, src, ACT.Copy)

            def split_x(g, par, half, chunks=range(CH)):
                n = 2 * g + half
                for i in chunks:
                    act.wait_ge(x_in_sem[i], 16 * g + 16)
                    if not (isinstance(n, int) and n == 0):
                        act.wait_ge(x_used, CH * n + (i + 1 - CH))
                    copy(xs[0][:, KC * i:KC * (i + 1), :],
                         xraw[par][:, KC * i:KC * (i + 1), half * HALF:(half + 1) * HALF]).then_inc(x_hi, 1)

            def split_b(g):
                act.wait_ge(gathered, 16 * 2 * GROUP * (g + 1))
                for q in QUARTERS:
                    copy(b_quarter(bst[0], q), b_raw(q)).then_inc(b_hi, 1)

            def split_a(g):
                act.wait_ge(gathered, 16 * 2 * GROUP * (g + 1))
                copy(a1s[0][:].rearrange("p k (b r) -> p b k r", b=GROUP), a_raw).then_inc(a_hi, 1)

            def h_and_k1(g):
                act.wait_ge(h_sum, 2 * g + 2)
                copy(hsb[:, 1, HROWS:HROWS + LR], hsb[:, 1, 0:LR]).then_inc(h_copied, 1)
                act.wait_ge(sel_done, g + 1)
                copy(k1[0][:], ps_s[:]).then_inc(k1_hi, 1)

            def c0_high(g):
                act.wait_ge(cm_done, g + 1)
                copy(c0s[0][:], cm[:]).then_inc(c0_hi, 1)

            act.wait_ge(a0_in, 16)
            copy(a0s[0][:].rearrange("p k n -> p (k n)"), a0raw).then_inc(a0_hi, 1)
            for k in range(KT):
                act.wait_ge(w0_in[k], 16)
                copy(w0s[0][:, k, 0:D], w0raw[k]).then_inc(w0_hi, 1)
            act.wait_ge(exp0_in, 16 * EXP)
            copy(exp0s[0].rearrange("p k (e c) -> p e k c", e=EXP), exp0_zl).then_inc(small_hi, 1)
            copy(hr_hi[:, :, P:P + LR].rearrange("p k (e r) -> p e k r", e=EXP), exp0_cols
                 ).then_inc(small_hi, 1)
            act.wait_ge(bias_step, 1)
            act.activation(cb[:, 1, :], cb[:, 0, :], ACT.Ln).then_inc(ln_done, 1)

            def m0_high(n):
                cols, at = WIDE_PARTS[n]
                width = min(cols.stop, D) - cols.start
                to = slice(cols.start, cols.start + width)
                copy(m0f[:, to], ps_d[at][:, 0:width]).then_inc(m0_copy, 1)
                if n == F_PART:
                    copy(f0s[:, 0, :], ps_d[at][:, F_AT:F_AT + FC])
                copy(m0s[0][:, to], ps_d[at][:, 0:width]).then_inc(m0_hi, 1)

            split_x(0, 0, 0, [0])
            act.wait_ge(m0_done, 1)
            for n in (0, 2):
                m0_high(n)
            act.wait_ge(ln_done, 1)
            act.activation(ex[:, 0, :], cb[:, 1, :], ACT.Exp)
            split_x(0, 0, 0, [1])
            act.wait_ge(m0_done, 2)
            m0_high(F_PART)
            split_x(0, 0, 0, [2])
            split_b(0)
            split_x(0, 0, 0, [3])
            act.wait_ge(m0t_done, 1)
            for h, src in enumerate((ps_s, ps_t)):
                copy(hr_hi[:, 4 * h:4 * h + 4, 0:P], src[:].rearrange("p (k n) -> p k n", n=P)
                     ).then_inc(m0t_hi, 1)
            for k in range(KT):
                if k == 1:
                    split_x(0, 0, 1, [0, 1])
                if k == 2:
                    split_x(0, 0, 1, [2, 3])
                if k == 3:
                    act.wait_ge(exp1_sem, 32)
                    copy(exp1_hi, exp1_raw).then_inc(small_hi, 1)
                    copy(hr_hi[:, :, P + LR:P + LR + 1], bia[:, 0, :].rearrange("p (k a) -> p k a", a=1)
                         ).then_inc(small_hi, 1)
                    split_a(0)
                if k == 5:
                    c0_high(0)
                if k == 7:
                    h_and_k1(0)
                act.wait_ge(w1_in[k], 16)
                copy(w1s[0][:, k, 0:D], w1raw[k]).then_inc(w1_hi, 1)

            def experts_high():
                act.wait_ge(rows_in, 16 * (EXP + 1))
                for half in range(2):
                    copy(m1x[0][L0ROWS[half], half, :], rows_raw[L0ROWS[0], :]).then_inc(rows_hi, 1)

            def body(g, par, last):
                first = isinstance(g, int) and g == 0
                if not first:
                    h_and_k1(g)
                if not last and not first:
                    split_b(g + 1)

                def wide_high(n):
                    cols, at = WIDE_PARTS[n]
                    width = min(cols.stop, D) - cols.start
                    act.wait_ge(m1_done, 3 * g + n + 1)
                    for half in range(2):
                        if n == F_PART:
                            copy(f1s[L1ROWS[half], half, 0, :], ps_d[at][L1ROWS[half], F_AT:F_AT + FC])
                        copy(m1x[0][L1ROWS[half], half, cols.start:cols.start + width],
                             ps_d[at][L1ROWS[half], 0:width]).then_inc(m1_hi, 1)

                def coef_high(layer):
                    act.wait_ge(t_done, 2 * g + layer + 1)
                    for half in range(2):
                        rows, cols = (E0ROWS, E1ROWS)[layer][half], slice(half * HALF, (half + 1) * HALF)
                        copy(k2[0][rows, cols], ps_t[rows, cols]).then_inc(l_hi, 1)

                def softmax_exp(layer):
                    act.wait_ge(sm_step, 9 * g + 4 * layer + 3)
                    act.activation(ex[:], lg[:], ACT.Exp).then_inc(exp_done, 1)

                wide_high(0)
                act.wait_ge(ht_done, g + 1)
                copy(hts[0][:], ps_t[:, 0:P]).then_inc(ht_hi, 1)
                for half in range(2):
                    rows = E0ROWS[half]
                    copy(hls[0][rows, half, :], ps_t[rows, P:2 * P]).then_inc(ht_hi, 1)
                if not last and not first:
                    split_x(g + 1, 1 - par, 0, [0, 1])
                softmax_exp(0)
                if first:
                    experts_high()
                wide_high(1)
                coef_high(0)
                if first:
                    split_x(g + 1, 1 - par, 0, [0])
                    split_b(g + 1)
                    split_x(g + 1, 1 - par, 0, [1])
                if not last:
                    split_x(g + 1, 1 - par, 0, [2, 3])
                wide_high(2)
                if not last:
                    split_x(g + 1, 1 - par, 1, [0])
                act.wait_ge(c1_done, 2 * g + 1)
                for half in range(2):
                    cols = slice(half * HALF, (half + 1) * HALF)
                    if half == 1:
                        act.wait_ge(c1_done, 2 * g + 2)
                    copy(k2[0][L1ROWS[half], cols], cm[L1ROWS[half], cols]).then_inc(c1_hi, 1)
                if not last:
                    split_x(g + 1, 1 - par, 1, range(1, CH))
                softmax_exp(1)
                if not last:
                    split_a(g + 1)
                coef_high(1)
                if not last:
                    c0_high(g + 1)

            steps(act, body)

        @block.vector
        def _(dve):
            def low(dst, whole, high):
                return dve.tensor_tensor(dst, whole, high.bitcast(F32), ALU.subtract)

            def masked(g):
                dve.wait_ge(x_used, 2 * CH * (g + 1))
                dve.tensor_tensor(cm[:].rearrange("p (a t) -> p a t", a=2),
                                  ps_p[:].rearrange("p (a t) -> p a t", a=2), mask, ALU.mult
                                  ).then_inc(cm_done, 1)

            def select(g):
                after_step(dve, sel_done, g)
                for half in range(2):
                    dve.tensor_scalar(sel[:, half, :], adapter_of, idf[:, half, bass.ds(g, 1)], None,
                                      ALU.is_equal).then_inc(sel_built, 1)

            def h_to_sbuf(g):
                whole = hsb[:].rearrange("p a n -> p (a n)")
                dve.wait_ge(h_done, g + 1)
                for half in range(2):
                    dve.tensor_reduce(whole[L1ROWS[half], 0:HC],
                                      ps_h[L1ROWS[1 - half], 0:2 * HC].rearrange("p (a n) -> p n a", a=2),
                                      AX.X, ALU.add).then_inc(h_sum, 1)

            def k1_low(g):
                dve.wait_ge(k1_hi, g + 1)
                low(k1[1][:], ps_s[:], k1[0][:]).then_inc(k1_lo, 1)

            def c0_low(g):
                dve.wait_ge(c0_hi, g + 1)
                low(c0s[1][:], cm[:], c0s[0][:]).then_inc(c0_lo, 1)

            def split_b(g):
                for n, q in enumerate(QUARTERS):
                    dve.wait_ge(b_hi, 4 * g + n + 1)
                    low(b_quarter(bst[1], q), b_raw(q), b_quarter(bst[0], q)).then_inc(b_lo, 1)

            def split_x_odd(g, par, chunks):
                for i in chunks:
                    dve.wait_ge(x_hi, 2 * CH * g + CH + i + 1)
                    low(xs[1][:, KC * i:KC * (i + 1), :], xraw[par][:, KC * i:KC * (i + 1), HALF:],
                        xs[0][:, KC * i:KC * (i + 1), :]).then_inc(x_lo_dve, 1)

            for t in (*hls, f1s, *k2):
                dve.memset(t[:].bitcast(F32), 0.0)
            dve.memset(hr[:, :, :, HC - 1:HC].bitcast(F32), 0.0)
            dve.memset(hsb[:, 1, :], 0.0).then_inc(init_done, 1)
            dve.wait_ge(a0_hi, 1)
            low(a0s[1][:].rearrange("p k n -> p (k n)"), a0raw, a0s[0][:].rearrange("p k n -> p (k n)")
                ).then_inc(a0_lo, 1)
            for k in range(KT):
                dve.wait_ge(w0_hi, k + 1)
                low(w0s[1][:, k, 0:D], w0raw[k], w0s[0][:, k, 0:D]).then_inc(w0_lo, 1)
            dve.wait_ge(small_hi, 2)
            dve.tensor_scalar(cb[:, 0, :], exp0_prior, EPS, None, ALU.add).then_inc(bias_step, 1)
            low(exp0s[1].rearrange("p k (e c) -> p e k c", e=EXP), exp0_zl,
                exp0s[0].rearrange("p k (e c) -> p e k c", e=EXP)).then_inc(small_lo, 1)
            low(hr_lo[:, :, P:P + LR].rearrange("p k (e r) -> p e k r", e=EXP), exp0_cols,
                hr_hi[:, :, P:P + LR].rearrange("p k (e r) -> p e k r", e=EXP)).then_inc(small_lo, 1)
            for i, n in enumerate((0, 2, F_PART)):
                cols, at = WIDE_PARTS[n]
                width = min(cols.stop, D) - cols.start
                to = slice(cols.start, cols.start + width)
                dve.wait_ge(m0_hi, i + 1)
                if n == F_PART:
                    low(f0s[:, 1, :], ps_d[at][:, F_AT:F_AT + FC], f0s[:, 0, :])
                low(m0s[1][:, to], ps_d[at][:, 0:width], m0s[0][:, to]).then_inc(m0_lo, 1)
            split_b(0)
            for h, src in enumerate((ps_s, ps_t)):
                dve.wait_ge(m0t_hi, h + 1)
                low(hr_lo[:, 4 * h:4 * h + 4, 0:P], src[:].rearrange("p (k n) -> p k n", n=P),
                    hr_hi[:, 4 * h:4 * h + 4, 0:P]).then_inc(m0t_lo, 1)
            dve.wait_ge(marks_in, 32)
            dve.tensor_copy(idf[:], idi[:]).then_inc(bias_step, 1)
            for k in range(KT):
                if k in (1, 2):
                    split_x_odd(0, 0, [2 * k - 1])
                if k == 3:
                    dve.wait_ge(small_hi, 4)
                    low(exp1_lo, exp1_raw, exp1_hi).then_inc(small_lo, 1)
                    low(hr_lo[:, :, P + LR:P + LR + 1], bia[:, 0, :].rearrange("p (k a) -> p k a", a=1),
                        hr_hi[:, :, P + LR:P + LR + 1]).then_inc(small_lo, 1)
                if k == 4:
                    dve.wait_ge(bias_step, 2)
                    dve.wait_ge(small_lo, 3)
                    masked(0)
                    select(0)
                    h_to_sbuf(0)
                    c0_low(0)
                if k == 7:
                    k1_low(0)
                if k == POOL_CHUNK:
                    continue
                dve.wait_ge(w1_hi, k + 1)
                low(w1s[1][:, k, 0:D], w1raw[k], w1s[0][:, k, 0:D]).then_inc(w1_lo, 1)

            def routing_constants():
                dve.tensor_tensor(bsum[:], bia[:, 0, :], bia[:, 1, :], ALU.add).then_inc(bias_step, 1)
                dve.wait_ge(ln_done, 1)
                dve.tensor_tensor(cb[:, 0, :], cb[:, 1, :], exp0_routerb, ALU.add).then_inc(bias_step, 1)
                dve.wait_ge(bias_step, 4)
                dve.memset(lp[:], 0.0).then_inc(init_done, 1)
                dve.wait_ge(init_done, 2)

            def experts_low():
                dve.wait_ge(rows_hi, 2)
                for half in range(2):
                    low(m1x[1][L0ROWS[half], half, :], rows_raw[L0ROWS[0], :], m1x[0][L0ROWS[0], 0, :]
                        ).then_inc(rows_lo, 1)

            def body(g, par, last):
                first = isinstance(g, int) and g == 0
                if not first:
                    h_to_sbuf(g)
                    k1_low(g)
                if not last and not first:
                    split_b(g + 1)

                def wide_low(n):
                    cols, at = WIDE_PARTS[n]
                    width = min(cols.stop, D) - cols.start
                    to = slice(cols.start, cols.start + width)
                    for half in range(2):
                        dve.wait_ge(m1_hi, 6 * g + 2 * n + half + 1)
                        low(m1x[1][L1ROWS[half], half, to], ps_d[at][L1ROWS[half], 0:width],
                            m1x[0][L1ROWS[half], half, to]).then_inc(m1_lo, 1)
                        if n == F_PART:
                            low(f1s[L1ROWS[half], half, 1, :], ps_d[at][L1ROWS[half], F_AT:F_AT + FC],
                                f1s[L1ROWS[half], half, 0, :]).then_inc(f1_lo, 1)

                def coef_low(layer):
                    for half in range(2):
                        rows, cols = (E0ROWS, E1ROWS)[layer][half], slice(half * HALF, (half + 1) * HALF)
                        dve.wait_ge(l_hi, 4 * g + 2 * layer + half + 1)
                        low(k2[1][rows, cols], ps_t[rows, cols], k2[0][rows, cols]).then_inc(l_lo, 1)

                def softmax(layer):
                    at = 9 * g + (4 if layer else 0)
                    dve.wait_ge(z_done, 2 * g + layer + 1)
                    dve.tensor_reduce(zs, ps_z[:, 0:TT * 2 * FC].rearrange("p (j a e c) -> p j e c a", j=TT,
                                                                           a=2, e=EXP),
                                      AX.X, ALU.add).then_inc(z_sum, 1)
                    dve.wait_ge(z_sum, 2 * g + layer + 1)
                    logits = zs[:, :, :, ER]
                    if layer == 0:
                        dve.tensor_tensor(lg[:], logits, cb[:, 0:1, :].to_broadcast([P, TT, EXP]), ALU.add
                                          ).then_inc(sm_step, 1)
                        dve.wait_ge(sm_step, at + 1)
                        logits = lg[:]
                    dve.tensor_reduce(mx[:], logits, AX.X, ALU.max).then_inc(sm_step, 1)
                    dve.wait_ge(sm_step, at + 2)
                    dve.tensor_tensor(lg[:], logits,
                                      mx[:].rearrange("p (j a) -> p j a", a=1).to_broadcast([P, TT, EXP]),
                                      ALU.subtract).then_inc(sm_step, 1)
                    if layer == 1 and not last:
                        split_x_odd(g + 1, 1 - par, [3])
                    dve.wait_ge(exp_done, 2 * g + layer + 1)
                    dve.tensor_reduce(rs[:, 0, :], ex[:], AX.X, ALU.add).then_inc(sm_step, 1)
                    dve.wait_ge(sm_step, at + 4)
                    dve.reciprocal(rs[:, 1, :], rs[:, 0, :]).then_inc(sm_step, 1)
                    dve.wait_ge(sm_step, at + 5)
                    dve.scalar_tensor_tensor(out=lg[:], in0=ex[:], scalar=2.0,
                                             in1=rs[:, 1, :].rearrange("p (j a) -> p j a", a=1)
                                             .to_broadcast([P, TT, EXP]),
                                             op0=ALU.mult, op1=ALU.mult).then_inc(alpha_done, 1)
                    dve.wait_ge(alpha_done, 2 * g + layer + 1)
                    to = lp[:, HROWS:HROWS + TT * P].rearrange("p (j e r) -> p j e r", j=TT, r=ER)[
                        :, :, layer * EXP:(layer + 1) * EXP, :]
                    dve.tensor_tensor(to, zs[:, :, :, 0:ER],
                                      lg[:].rearrange("p j (e a) -> p j e a", a=1)
                                      .to_broadcast([P, TT, EXP, ER]), ALU.mult).then_inc(l_done, 1)

                wide_low(0)
                dve.wait_ge(ht_hi, 3 * g + 3)
                low(hts[1][:], ps_t[:, 0:P], hts[0][:])
                for half in range(2):
                    rows = E0ROWS[half]
                    ins = low(hls[1][rows, half, :], ps_t[rows, P:2 * P], hls[0][rows, half, :])
                ins.then_inc(ht_lo, 1)
                if first:
                    routing_constants()
                softmax(0)
                if first:
                    experts_low()
                wide_low(1)
                coef_low(0)
                if first:
                    split_b(g + 1)
                dve.wait_ge(q_done, g + 1)
                for half in range(2):
                    cols = slice(half * HALF, (half + 1) * HALF)
                    dve.scalar_tensor_tensor(out=ps_s[:, cols], in0=ps_s[:, cols], scalar=hb,
                                             in1=mark[:, 0:HALF], op0=ALU.add, op1=ALU.mult
                                             ).then_inc(qm_done, 1)
                    dve.wait_ge(qm_done, 2 * g + half + 1)
                    dve.tensor_tensor(cm[:, cols], cm[:, cols], ps_s[:, cols], ALU.add).then_inc(c1_done, 1)
                for half in range(2):
                    cols = slice(half * HALF, (half + 1) * HALF)
                    dve.wait_ge(c1_hi, 2 * g + half + 1)
                    low(k2[1][L1ROWS[half], cols], cm[L1ROWS[half], cols], k2[0][L1ROWS[half], cols]
                        ).then_inc(c1_lo, 1)
                if not last:
                    split_x_odd(g + 1, 1 - par, [1])
                if last:
                    wide_low(2)
                softmax(1)
                if not last:
                    wide_low(2)
                coef_low(1)
                if not last:
                    masked(g + 1)
                banks = result_banks(last)
                for m in range(KT):
                    dve.wait_ge(d_done, KT * g + m + 1)
                    dve.scalar_tensor_tensor(out=xraw[par][:, m, :], in0=banks[m % len(banks)][:],
                                             scalar=bsum[:, m:m + 1], in1=xraw[par][:, m, :],
                                             op0=ALU.add, op1=ALU.add).then_inc(d_out, 1)
                    if not last and m == 1:
                        select(g + 1)
                    if not last and m == 2:
                        c0_low(g + 1)

            steps(dve, body)

        @block.gpsimd
        def _(pool):
            def low(dst, whole, high):
                return pool.tensor_tensor(dst, whole, high.bitcast(F32), ALU.subtract)

            def split_x(g, par, half, chunks):
                for i in chunks:
                    pool.wait_ge(x_hi, 2 * CH * g + CH * half + i + 1)
                    low(xs[1][:, KC * i:KC * (i + 1), :],
                        xraw[par][:, KC * i:KC * (i + 1), half * HALF:(half + 1) * HALF],
                        xs[0][:, KC * i:KC * (i + 1), :]).then_inc(x_lo, 1)

            def split_a(g):
                pool.wait_ge(a_hi, g + 1)
                low(a1s[1][:].rearrange("p k (b r) -> p b k r", b=GROUP), a_raw,
                    a1s[0][:].rearrange("p k (b r) -> p b k r", b=GROUP)).then_inc(a_lo, 1)

            split_x(0, 0, 0, range(CH))
            split_x(0, 0, 1, (0, 2))
            split_a(0)
            pool.wait_ge(w1_hi, POOL_CHUNK + 1)
            low(w1s[1][:, POOL_CHUNK, 0:D], w1raw[POOL_CHUNK], w1s[0][:, POOL_CHUNK, 0:D]
                ).then_inc(w1_lo_pool, 1)

            def body(g, par, last):
                if not last:
                    split_x(g + 1, 1 - par, 0, range(CH))
                    split_x(g + 1, 1 - par, 1, (0, 2))
                    split_a(g + 1)

            steps(pool, body)


def kernel(x, itok_B_3_7, itok_B_4_50, L0_cond_A, L0_cond_B, L0_ffn_W_base, L0_ffn_b_base, L0_ffn_lora_A,
           L0_ffn_lora_B, L0_ffn_router_W, L0_ffn_router_b, L0_ffn_domain_prior, L0_ffn_active, L1_cond_A,
           L1_cond_B, L1_ffn_W, L1_ffn_b, L1_ffn_A, L1_ffn_Bm, L1_ffn_Wr):
    import numpy as np
    import concourse.bacc as bacc
    from concourse.bass_utils import run_bass_kernel_spmd

    x, id0, id1, A0, B0, W0, b0, EA, EB, RW, Rb, prior, active, A1, B1, W1, b1, LA, LB, WR = (
        np.asarray(a) for a in (
            x, itok_B_3_7, itok_B_4_50, L0_cond_A, L0_cond_B, L0_ffn_W_base, L0_ffn_b_base, L0_ffn_lora_A,
            L0_ffn_lora_B, L0_ffn_router_W, L0_ffn_router_b, L0_ffn_domain_prior, L0_ffn_active, L1_cond_A,
            L1_cond_B, L1_ffn_W, L1_ffn_b, L1_ffn_A, L1_ffn_Bm, L1_ffn_Wr))

    def tiles(a):
        return np.swapaxes(a.reshape(*a.shape[:-1], KT, P), -1, -2)

    n_exp = EA.shape[0]
    rows = np.arange(P)
    seq_of_row, seq_of_col = rows % HROWS // RANK, np.arange(HALF) // LEN
    marks = np.concatenate([
        seq_of_row[:, None] == seq_of_col[None, :],
        np.where(rows[:, None] % RANK == rows[None, :] % RANK, rows[None, :] // RANK, -2),
    ], axis=1).astype(mybir.dt.np(BF16))
    row_ids = np.repeat(id0.reshape(STEPS, 2, HSEQ).transpose(1, 2, 0), RANK, axis=1)
    none = np.full_like(row_ids[0], -1)
    named = {
        "x_in": x.reshape(STEPS, TOK, KT, P).transpose(0, 3, 2, 1),
        "id0_row": np.stack([np.concatenate([none, row_ids[0]]), np.concatenate([row_ids[1], none])], axis=1),
        "all_ids": np.concatenate([id0, id1, active]).reshape(1, -1),
        "a0": tiles(A0.transpose(0, 2, 1)).transpose(2, 3, 0, 1).reshape(P, -1),
        "b0_tab": tiles(B0).transpose(0, 2, 3, 1).reshape(ADAPT0, P, -1),
        "ab1_tab": np.concatenate([tiles(B1).transpose(0, 2, 3, 1).reshape(SEQS, P, -1),
                                   A1.reshape(SEQS, KT, P, RANK).transpose(0, 2, 1, 3).reshape(SEQS, P, -1)],
                                  axis=2),
        "w0": W0.T.reshape(KT, P, D),
        "w1": W1.T.reshape(KT, P, D),
        "exp0": np.concatenate([
            tiles(np.concatenate([EA, RW[:, None, :]], axis=1)).transpose(0, 2, 3, 1).reshape(n_exp, P, -1),
            EB.reshape(n_exp, KT, P, ER).transpose(0, 2, 1, 3).reshape(n_exp, P, -1),
            np.repeat(np.stack([Rb, prior], axis=1)[:, None, :], P, axis=1)], axis=2),
        "exp0_rows": EB.transpose(0, 2, 1),
        "exp1_in": tiles(np.concatenate([LA, WR[:, None, :]], axis=1)).transpose(2, 3, 0, 1).reshape(P, -1),
        "exp1_rows": LB.transpose(0, 2, 1).reshape(LR, D),
        "bias": tiles(np.stack([b0, b1])).transpose(1, 0, 2),
        "identity": np.eye(P, dtype=np.float32),
        "marks": marks,
    }
    nc = bacc.Bacc("TRN2", target_bir_lowering=False, num_devices=1)
    arrays, args = {}, []
    for name, a in named.items():
        a = np.ascontiguousarray(a)
        arrays[name] = a
        args.append(nc.dram_tensor(name, a.shape, mybir.dt.from_np(a.dtype), kind="ExternalInput").ap())
    out = nc.dram_tensor("out", (STEPS, P, KT, TOK), F32, kind="ExternalOutput").ap()
    two_layer_adapter_lora(nc, *args, out)
    r = run_bass_kernel_spmd(nc, [arrays], core_ids=[0])
    y = r.results[0]["out"].reshape(STEPS, P, KT, TOK)
    return y.transpose(0, 3, 2, 1).reshape(SEQS, LEN, D)
```
